# Optimizing a Trainium2 kernel written in Bass

```python
import numpy as np
import jax
import jax.numpy as jnp

def _softmax(x, axis=-1):
    return jax.nn.softmax(x, axis=axis)

def _gelu(x):
    return jax.nn.gelu(x, approximate=True)

def _silu(x):
    return jax.nn.silu(x)

def _sigmoid(x):
    return jax.nn.sigmoid(x)

def _layernorm(x, axis=-1, eps=1e-05):
    m = jnp.mean(x, axis=axis, keepdims=True)
    v = jnp.var(x, axis=axis, keepdims=True)
    return (x - m) / jnp.sqrt(v + eps)

def _scatter_add(tgt, idx, src, axis=0):
    return tgt.at[idx].add(src)

def _segment_sum(src, seg, n):
    return jax.ops.segment_sum(src, seg, n)
kernel_name = 'mk_gnn_ffn_d2_gnn_r8_2f459b'

def setup_inputs(seed: int=0):
    np.random.seed(seed)
    _w = jnp.asarray

    def _rec_inputs():
        import jax
        import jax.numpy as jnp
        _gk = jax.random.key(seed)
        x = -0.0003713 + 1 * jax.random.normal(jax.random.fold_in(_gk, 1), (6250, 256), jnp.float32)
        src = jax.random.randint(jax.random.fold_in(_gk, 2), (200000,), 0, 6250, jnp.int32)
        dst = jnp.minimum((6250 * jax.random.uniform(jax.random.fold_in(_gk, 3), (200000,)) ** 2.0).astype(jnp.int32), 49999)
        _o = jnp.argsort(dst, stable=True)
        src = src[_o]
        dst = dst[_o]
        return (x, src, dst)
    x, src, dst = _rec_inputs()

    def _L0_gnn_setup():
        import jax, jax.numpy as jnp
        import numpy as np
        N, E, H, D = (6250, 100000, 4, 64)
        IN_DIM = H * D
        NEG_SLOPE = 0.2
        key = jax.random.key(seed)
        k = jax.random.split(key, 7)
        h = jax.random.normal(k[0], (N, IN_DIM), dtype=jnp.float32)
        W = jax.random.normal(k[1], (IN_DIM, H * D), dtype=jnp.float32) * (1.0 / np.sqrt(IN_DIM))
        attn_l = jax.random.normal(k[2], (H, D), dtype=jnp.float32) * 0.1
        attn_r = jax.random.normal(k[3], (H, D), dtype=jnp.float32) * 0.1
        bias = jnp.zeros((H * D,), dtype=jnp.float32)
        src = jax.random.randint(k[4], (E,), 0, N, dtype=jnp.int32)
        dst = jax.random.randint(k[5], (E,), 0, N, dtype=jnp.int32)
        return {'h': h, 'W': W, 'attn_l': attn_l, 'attn_r': attn_r, 'bias': bias, 'src': src, 'dst': dst}
    _L0_gnn_all = _L0_gnn_setup()
    _L0_gnn_in = {k: v for k, v in _L0_gnn_all.items() if k in ('W', 'attn_l', 'attn_r', 'bias')}
    del _L0_gnn_all

    def _L0_ffn_setup():
        import math
        import jax, jax.numpy as jnp
        import numpy as np
        CAPACITY_FACTOR = 1.25
        key = jax.random.key(seed)
        ks = jax.random.split(key, 5)
        B, L, D, F, E = (8, 1024, 256, 1024, 8)
        h = jax.random.normal(ks[0], (B, L, D), dtype=jnp.float32)
        gate_w = jax.random.normal(ks[1], (D, E), dtype=jnp.float32) * 0.02
        gate_b = jnp.zeros((E,), dtype=jnp.float32)
        w1 = jax.random.normal(ks[2], (E, D, F), dtype=jnp.float32) * (1.0 / math.sqrt(D))
        b1 = jnp.zeros((E, F), dtype=jnp.float32)
        w2 = jax.random.normal(ks[3], (E, F, D), dtype=jnp.float32) * (1.0 / math.sqrt(F))
        b2 = jnp.zeros((E, D), dtype=jnp.float32)
        return {'h': h, 'gate_w': gate_w, 'gate_b': gate_b, 'w1': w1, 'b1': b1, 'w2': w2, 'b2': b2}
    _L0_ffn_all = _L0_ffn_setup()
    _L0_ffn_in = {k: v for k, v in _L0_ffn_all.items() if k in ('gate_w', 'gate_b', 'w1', 'b1', 'w2', 'b2')}
    del _L0_ffn_all

    def _L1_gnn_setup():
        import jax, jax.numpy as jnp
        import numpy as np
        N = 6250
        E = 100000
        D = 256
        EPS = 1e-05

        def _gcn_norm(row, col, n):
            ew = jnp.ones(row.shape[0], jnp.float32)
            deg = jax.ops.segment_sum(ew, col, num_segments=n)
            dis = jnp.where(deg > 0, jax.lax.rsqrt(deg), 0.0)
            return dis[row] * dis[col]

        def _gcn_conv(z, W, b, row, col, n):
            norm = _gcn_norm(row, col, n)
            h = z @ W
            msg = h[row] * norm[:, None]
            return jax.ops.segment_sum(msg, col, num_segments=n) + b

        def _batchnorm(z, g, bt):
            mu = z.mean(axis=0)
            var = ((z - mu) ** 2).mean(axis=0)
            return g * (z - mu) * jax.lax.rsqrt(var + EPS) + bt
        key = jax.random.key(seed)
        ks = jax.random.split(key, 12)
        x = jax.random.normal(ks[0], (N, D), dtype=jnp.float32)
        row = jax.random.randint(ks[1], (E,), 0, N)
        col = jax.random.randint(ks[2], (E,), 0, N)
        col = jnp.where(col == row, (col + 1) % N, col)
        edge_index = jnp.stack([row, col]).astype(jnp.int64)
        s = 1.0 / np.sqrt(D)
        return {'x': x, 'edge_index': edge_index, 'W0': jax.random.normal(ks[3], (D, D), dtype=jnp.float32) * s, 'b0': jnp.zeros((D,), jnp.float32), 'g0': jnp.ones((D,), jnp.float32), 'bt0': jnp.zeros((D,), jnp.float32), 'W1': jax.random.normal(ks[4], (D, D), dtype=jnp.float32) * s, 'b1': jnp.zeros((D,), jnp.float32), 'g1': jnp.ones((D,), jnp.float32), 'bt1': jnp.zeros((D,), jnp.float32)}
    _L1_gnn_all = _L1_gnn_setup()
    _L1_gnn_in = {k: v for k, v in _L1_gnn_all.items() if k in ('W0', 'b0', 'g0', 'bt0', 'W1', 'b1', 'g1', 'bt1')}
    del _L1_gnn_all

    def _L1_ffn_setup():
        import jax, jax.numpy as jnp
        import numpy as np
        TOP_K = 2
        LN_EPS = 1e-05
        key = jax.random.key(seed)
        ks = jax.random.split(key, 8)
        B, S, D, E, H = (16, 1024, 256, 8, 1024)
        x = jax.random.normal(ks[0], (B, S, D), dtype=jnp.float32)
        Wr = jax.random.normal(ks[1], (D, E), dtype=jnp.float32) * 0.1
        br = jnp.zeros((E,), dtype=jnp.float32)
        ln_g = jnp.ones((E, D), dtype=jnp.float32)
        ln_b = jnp.zeros((E, D), dtype=jnp.float32)
        W1 = jax.random.normal(ks[2], (E, D, H), dtype=jnp.float32) * (1.0 / np.sqrt(D))
        b1 = jnp.zeros((E, H), dtype=jnp.float32)
        W2 = jax.random.normal(ks[3], (E, H, D), dtype=jnp.float32) * (1.0 / np.sqrt(H))
        b2 = jnp.zeros((E, D), dtype=jnp.float32)
        return {'x': x, 'Wr': Wr, 'br': br, 'ln_g': ln_g, 'ln_b': ln_b, 'W1': W1, 'b1': b1, 'W2': W2, 'b2': b2}
    _L1_ffn_all = _L1_ffn_setup()
    _L1_ffn_in = {k: v for k, v in _L1_ffn_all.items() if k in ('Wr', 'br', 'ln_g', 'ln_b', 'W1', 'b1', 'W2', 'b2')}
    del _L1_ffn_all
    return {'x': x, 'src': src, 'dst': dst, 'L0_gnn_W': _L0_gnn_in['W'], 'L0_gnn_attn_l': _L0_gnn_in['attn_l'], 'L0_gnn_attn_r': _L0_gnn_in['attn_r'], 'L0_gnn_bias': _L0_gnn_in['bias'], 'L0_ffn_gate_w': _L0_ffn_in['gate_w'], 'L0_ffn_gate_b': _L0_ffn_in['gate_b'], 'L0_ffn_w1': _L0_ffn_in['w1'], 'L0_ffn_b1': _L0_ffn_in['b1'], 'L0_ffn_w2': _L0_ffn_in['w2'], 'L0_ffn_b2': _L0_ffn_in['b2'], 'L1_gnn_W0': _L1_gnn_in['W0'], 'L1_gnn_b0': _L1_gnn_in['b0'], 'L1_gnn_g0': _L1_gnn_in['g0'], 'L1_gnn_bt0': _L1_gnn_in['bt0'], 'L1_gnn_W1': _L1_gnn_in['W1'], 'L1_gnn_b1': _L1_gnn_in['b1'], 'L1_gnn_g1': _L1_gnn_in['g1'], 'L1_gnn_bt1': _L1_gnn_in['bt1'], 'L1_ffn_Wr': _L1_ffn_in['Wr'], 'L1_ffn_br': _L1_ffn_in['br'], 'L1_ffn_ln_g': _L1_ffn_in['ln_g'], 'L1_ffn_ln_b': _L1_ffn_in['ln_b'], 'L1_ffn_W1': _L1_ffn_in['W1'], 'L1_ffn_b1': _L1_ffn_in['b1'], 'L1_ffn_W2': _L1_ffn_in['W2'], 'L1_ffn_b2': _L1_ffn_in['b2']}

def reference(x, src, dst, L0_gnn_W, L0_gnn_attn_l, L0_gnn_attn_r, L0_gnn_bias, L0_ffn_gate_w, L0_ffn_gate_b, L0_ffn_w1, L0_ffn_b1, L0_ffn_w2, L0_ffn_b2, L1_gnn_W0, L1_gnn_b0, L1_gnn_g0, L1_gnn_bt0, L1_gnn_W1, L1_gnn_b1, L1_gnn_g1, L1_gnn_bt1, L1_ffn_Wr, L1_ffn_br, L1_ffn_ln_g, L1_ffn_ln_b, L1_ffn_W1, L1_ffn_b1, L1_ffn_W2, L1_ffn_b2):
    import jax
    import jax.numpy as jnp

    def _L0_gnn_ref(h, W, attn_l, attn_r, bias, src, dst):
        import jax, jax.numpy as jnp
        import numpy as np
        N, E, H, D = (6250, 100000, 4, 64)
        IN_DIM = H * D
        NEG_SLOPE = 0.2
        feat = (h @ W).reshape(N, H, D)
        el = jnp.einsum('nhd,hd->nh', feat, attn_l)
        er = jnp.einsum('nhd,hd->nh', feat, attn_r)
        e = jax.nn.leaky_relu(el[src] + er[dst], NEG_SLOPE)
        emax = jax.ops.segment_max(e, dst, num_segments=N)
        ex = jnp.exp(e - emax[dst])
        denom = jax.ops.segment_sum(ex, dst, num_segments=N)
        alpha = ex / denom[dst]
        msg = feat[src] * alpha[..., None]
        rst = jax.ops.segment_sum(msg, dst, num_segments=N)
        rst = rst + bias.reshape(1, H, D)
        out = jax.nn.elu(rst.reshape(N, H * D))
        return h + out

    def _L0_ffn_ref(h, gate_w, gate_b, w1, b1, w2, b2):
        import math
        import jax, jax.numpy as jnp
        import numpy as np
        CAPACITY_FACTOR = 1.25
        B, L, D = h.shape
        E = gate_w.shape[1]
        T = B * L
        C = max(1, math.ceil(CAPACITY_FACTOR * T / E))
        x = h.reshape(T, D)
        logits = x @ gate_w + gate_b
        probs = jax.nn.softmax(logits, axis=-1)
        idx = jnp.argmax(probs, axis=-1)
        prb = jnp.take_along_axis(probs, idx[:, None], axis=1)[:, 0]
        one_hot = jax.nn.one_hot(idx, E, dtype=jnp.float32)
        pos = (jnp.cumsum(one_hot, axis=0) * one_hot).sum(-1).astype(jnp.int32) - 1
        kept = pos < C
        pos_safe = jnp.where(kept, pos, C)
        buf = jnp.zeros((E, C, D), dtype=h.dtype).at[idx, pos_safe].set(x, mode='drop')
        hmid = jax.nn.relu(jnp.einsum('ecd,edf->ecf', buf, w1) + b1[:, None, :])
        ybuf = jnp.einsum('ecf,efd->ecd', hmid, w2) + b2[:, None, :]
        pos_g = jnp.minimum(pos, C - 1)
        y_tok = ybuf[idx, pos_g] * (prb * kept)[:, None]
        y = y_tok.reshape(B, L, D)
        y = jnp.nan_to_num(y, nan=0.0, posinf=10000.0, neginf=-10000.0)
        return y

    def _L1_gnn_ref(x, edge_index, W0, b0, g0, bt0, W1, b1, g1, bt1):
        import jax, jax.numpy as jnp
        import numpy as np
        N = 6250
        E = 100000
        D = 256
        EPS = 1e-05

        def _gcn_norm(row, col, n):
            ew = jnp.ones(row.shape[0], jnp.float32)
            deg = jax.ops.segment_sum(ew, col, num_segments=n)
            dis = jnp.where(deg > 0, jax.lax.rsqrt(deg), 0.0)
            return dis[row] * dis[col]

        def _gcn_conv(z, W, b, row, col, n):
            norm = _gcn_norm(row, col, n)
            h = z @ W
            msg = h[row] * norm[:, None]
            return jax.ops.segment_sum(msg, col, num_segments=n) + b

        def _batchnorm(z, g, bt):
            mu = z.mean(axis=0)
            var = ((z - mu) ** 2).mean(axis=0)
            return g * (z - mu) * jax.lax.rsqrt(var + EPS) + bt
        n = x.shape[0]
        loops = jnp.arange(n, dtype=edge_index.dtype)
        row = jnp.concatenate([edge_index[0], loops])
        col = jnp.concatenate([edge_index[1], loops])
        z = _gcn_conv(x, W0, b0, row, col, n)
        z = _batchnorm(jax.nn.relu(z), g0, bt0)
        z = _gcn_conv(z, W1, b1, row, col, n)
        z = _batchnorm(jax.nn.relu(z), g1, bt1)
        return z

    def _L1_ffn_ref(x, Wr, br, ln_g, ln_b, W1, b1, W2, b2):
        import jax, jax.numpy as jnp
        import numpy as np
        TOP_K = 2
        LN_EPS = 1e-05
        B, S, D = x.shape
        N = B * S
        xt = x.reshape(N, D)
        logits = xt @ Wr + br
        probs = jax.nn.softmax(logits, axis=-1)
        top_p, top_idx = jax.lax.top_k(probs, TOP_K)
        weights = top_p / top_p.sum(axis=-1, keepdims=True)
        mu = xt.mean(axis=-1, keepdims=True)
        var = ((xt - mu) ** 2).mean(axis=-1, keepdims=True)
        xn = (xt - mu) * jax.lax.rsqrt(var + LN_EPS)
        xe = xn[None, :, :] * ln_g[:, None, :] + ln_b[:, None, :]
        h = jax.nn.gelu(jnp.einsum('end,edh->enh', xe, W1) + b1[:, None, :], approximate=False)
        y = jnp.einsum('enh,ehd->end', h, W2) + b2[:, None, :]
        y_tok = jnp.transpose(y, (1, 0, 2))
        sel = jnp.take_along_axis(y_tok, top_idx[:, :, None], axis=1)
        out = (weights[:, :, None] * sel).sum(axis=1)
        return out.reshape(B, S, D)
    edge_index = jnp.stack([src, dst])
    x = x + _L0_gnn_ref(_layernorm(x, axis=-1), L0_gnn_W, L0_gnn_attn_l, L0_gnn_attn_r, L0_gnn_bias, src, dst)
    x = x + _L0_ffn_ref(_layernorm(x, axis=-1)[None], L0_ffn_gate_w, L0_ffn_gate_b, L0_ffn_w1, L0_ffn_b1, L0_ffn_w2, L0_ffn_b2)[0]
    x = x + _L1_gnn_ref(_layernorm(x, axis=-1), edge_index, L1_gnn_W0, L1_gnn_b0, L1_gnn_g0, L1_gnn_bt0, L1_gnn_W1, L1_gnn_b1, L1_gnn_g1, L1_gnn_bt1)
    x = x + _L1_ffn_ref(_layernorm(x, axis=-1)[None], L1_ffn_Wr, L1_ffn_br, L1_ffn_ln_g, L1_ffn_ln_b, L1_ffn_W1, L1_ffn_b1, L1_ffn_W2, L1_ffn_b2)[0]
    return x

_drawn_inputs = setup_inputs


def setup_inputs(seed=0):
    import zlib

    import numpy as np

    out = dict(_drawn_inputs(seed))
    spreads = {'L0_gnn_bias': (0.0, 0.1),
     'L0_ffn_gate_b': (0.0, 0.1),
     'L0_ffn_b1': (0.0, 0.535),
     'L0_ffn_b2': (0.0, 0.404),
     'L1_gnn_b0': (0.0, 0.1),
     'L1_gnn_g0': (1.0, 0.2),
     'L1_gnn_bt0': (0.0, 0.1),
     'L1_gnn_b1': (0.0, 0.1),
     'L1_gnn_g1': (1.0, 0.2),
     'L1_gnn_bt1': (0.0, 0.1),
     'L1_ffn_br': (0.0, 0.1),
     'L1_ffn_ln_g': (1.0, 0.2),
     'L1_ffn_ln_b': (0.0, 0.339),
     'L1_ffn_b1': (0.0, 0.352),
     'L1_ffn_b2': (0.0, 0.1)}
    factors = {}
    for name, (base, spread) in spreads.items():
        noise = np.random.default_rng([zlib.crc32(name.encode()), seed]).standard_normal(out[name].shape)
        drawn = base * np.exp(spread * noise) if base else spread * noise
        out[name] = jnp.asarray(drawn.astype(out[name].dtype))
    for name, factor in factors.items():
        out[name] = (out[name] * factor).astype(out[name].dtype)
    return out
```

```python
import math
from contextlib import ExitStack

import numpy as np
import concourse.bass as bass
from concourse import mybir

F32 = mybir.dt.float32
I32 = mybir.dt.int32
ALU = mybir.AluOpType
ACT = mybir.ActivationFunctionType
AX_X = mybir.AxisListType.X
RMAX = bass.bass_isa.ReduceOp.max

P = 128
D = 256
KC = D // P
N = 6250
NT = math.ceil(N / P)
LAST = N - (NT - 1) * P
TB = 7
NG = NT // TB
HEADS = 4
HD = D // HEADS
E = 200000
EB = 256
NB = math.ceil(E / EB)
NBP = NB + 2
UN = 4
PAIRS = math.ceil((NB + NT - 1) / UN) * UN
STEPS = PAIRS // UN
PCH = math.ceil((PAIRS + UN) / P)
PCOL = PCH * P
AW = 264
GW = D + HEADS
MW = GW + 1
NE = 8
FF = 1024
FC = FF // P
CAP = math.ceil(1.25 * N / NE)
TILES0 = (N + NE * (P - 1)) // P
TILES1 = (2 * N + NE * (P - 1)) // P
TILES0 += TILES0 % 2
TILES1 += TILES1 % 2
LN_EPS = 1e-5
BIG = 1.0e9
FMAX = 3.4028234e38
assert NG * TB == NT


def wait(eng, sem, value):
    if isinstance(value, int) and value <= 0:
        return
    eng.wait_ge(sem, value)


def rolled(eng, count, body):
    body(0)
    with eng.Fori(1, count) as i:
        body(i)


class Chain:

    def __init__(self, eng, sem):
        self.eng, self.sem, self.n = eng, sem, 0

    def __call__(self, ins):
        self.n += 1
        ins.then_inc(self.sem, 1)
        self.eng.wait_ge(self.sem, self.n)


def build(nc, x, src, dst, g0_w, g0_al, g0_ar, g0_bias, f0_gw, f0_gb, f0_w1, f0_b1, f0_w2, f0_b2,
          g1_w0, g1_b0, g1_g0, g1_bt0, g1_w1, g1_b1, g1_g1, g1_bt1, f1_wr, f1_br, f1_lg, f1_lb,
          f1_w1, f1_b1, f1_w2, f1_b2, out):
    src_pad = nc.dram_tensor("src_pad", [NBP * EB], I32).ap()
    dst_pad = nc.dram_tensor("dst_pad", [NBP * EB], I32).ap()
    src_cols = nc.dram_tensor("src_cols", [P, PCOL * 2], I32).ap()
    dst_cols = nc.dram_tensor("dst_cols", [P, PCOL * 2], F32).ap()
    table0 = nc.dram_tensor("table0", [NT * P, GW], F32).ap()
    table1 = nc.dram_tensor("table1", [NT * P, D], F32).ap()
    expert_in = nc.dram_tensor("expert_in", [TILES1 * P, D], F32).ap()
    expert_out = nc.dram_tensor("expert_out", [TILES1 * P, D], F32).ap()

    def rows(a, lo, hi):
        return a[lo * P:hi * P, :].rearrange("(t p) d -> p t d", p=P)

    with ExitStack() as ctx:
        ctx.enter_context(nc.allow_non_contiguous_dma(reason="a few short index and bias loads"))

        def sb(name, shape, dt=F32):
            return ctx.enter_context(nc.sbuf_tensor(name, shape, dt))

        taken = []

        def sem(name):
            taken.append(nc.alloc_semaphore(name=name))
            return taken[-1]

        def reuse_semaphores():
            nc.clear_and_free_semaphores(taken)
            taken.clear()
            nc.all_engine_barrier()

        psum = [ctx.enter_context(nc.psum_tensor(f"bank{i}", [P, 512], F32)) for i in range(8)]

        xres = sb("xres", [P, NT, D])
        xflat = xres[:, :, :].rearrange("p t d -> p (t d)")
        arena = sb("arena", [P, 2 * NT * D + TB * D + 8])
        used = [0]

        def room(width):
            used[0] += width
            return arena[:, used[0] - width:used[0]]

        acc_flat = room(NT * AW)
        acc = acc_flat.rearrange("p (t d) -> p t d", t=NT)
        src_sb = room(PCOL * 2).bitcast(I32)
        dst_sb = room(PCOL * 2)
        onehot = room(UN * EB).rearrange("p (u j n) -> p u j n", u=UN, j=2)
        onehot_t = room(UN * EB).rearrange("p (u j n) -> p u j n", u=UN, j=2)
        got = room(UN * 2 * AW).rearrange("p (u j n) -> p u j n", u=UN, j=2)
        msg = room(UN * 2 * AW).rearrange("p (u j n) -> p u j n", u=UN, j=2)
        wproj = room(KC * AW).rearrange("p (c n) -> p c n", c=KC)
        wraw = room(KC * D).rearrange("p (c n) -> p c n", c=KC)
        attn = room(2 * D).rearrange("p (a n) -> p a n", a=2)
        bias_bc = room(D)
        er_at = used[0]
        er_u = room(NT * 8).rearrange("p (t n) -> p t n", t=NT)
        el_all = room(NT * HEADS).rearrange("p (t n) -> p t n", t=NT)
        y_all = arena[:, 0:NT * D]
        pick_a = arena[:, 0:NT * D].rearrange("p (t d) -> p t d", t=NT)
        pick_b = arena[:, NT * D:2 * NT * D].rearrange("p (t d) -> p t d", t=NT)
        clean_at = 2 * NT * D
        W2W = NE * FC * D
        w2_sb = arena[:, 0:W2W].rearrange("p (e c d) -> p e c d", e=NE, c=FC)
        w1_ring = arena[:, W2W:W2W + 2 * KC * FF].rearrange("p (s c f) -> p s c f", s=2, c=KC)
        b2_bc = arena[:, W2W + 2 * KC * FF:W2W + 2 * KC * FF + NE * D]

        ident = sb("ident", [P, P])
        ones = sb("ones", [P, P])
        tri = sb("tri", [P, P])
        iota_n = sb("iota_n", [P, P])
        rings = sb("rings", [P, TB * (D + AW)])
        y_ring = rings[:, 0:TB * D].rearrange("p (t d) -> p t d", t=TB)
        yt_ring = sb("yt_ring", [P, 3, D])
        stage_flat = rings[:, TB * D:]
        stage = stage_flat.rearrange("p (t d) -> p t d", t=TB)
        hmid = rings[:, 0:2 * FF].rearrange("p (s c n) -> p s c n", s=2, c=FC)
        x_in = rings[:, 2 * FF:2 * FF + 2 * D].rearrange("p (s d) -> p s d", s=2)
        y_out = rings[:, 2 * FF + 2 * D:2 * FF + 4 * D].rearrange("p (s d) -> p s d", s=2)
        b1_sb = sb("b1_sb", [P, NE, FC])
        lg_sb = sb("lg_sb", [P, KC, NE])
        lb_sb = sb("lb_sb", [P, KC, NE])
        route_at = used[0]
        bn_g = room(D)
        bn_b = room(D)
        stats = sb("stats", [P, NT, 6])
        lnt = sb("lnt", [P, 6, NT])
        mean, rstd, nmr = lnt[:, 0, :], lnt[:, 1, :], lnt[:, 2, :]
        dis = sb("dis", [P, NT])
        small = sb("small", [P, 64])
        eps = sb("eps", [P, 1])
        tile_one = sb("tile_one", [P, 1])
        valid = sb("valid", [P, NT])
        gate_w = sb("gate_w", [P, KC, NE])
        gate_b = sb("gate_b", [P, NE])
        iota_e = sb("iota_e", [P, NE])
        logit = sb("logit", [P, NT, NE])
        slot = sb("slot", [P, 4, NT], I32)
        wgt = sb("wgt", [P, 2, NT])
        idx_ring = sb("idx_ring", [P, 2 * TB], I32)
        tpack = sb("tpack", [1, STEPS], I32)
        tile_e = sb("tile_e", [1, P], I32)

        def cols(a, c):
            return a[:, c * P:(c + 1) * P]

        def own(a, v):
            return a[:, bass.ds(v, 1)]

        k_c, k_x, k_pad = sem("k_c"), sem("k_x"), sem("k_pad")
        with nc.Block() as block:
            @block.gpsimd
            def _(pool):
                link = Chain(pool, k_c)
                link(pool.memset(ident[:, :], 0.0))
                link(pool.affine_select(out=ident[:, :], in_=ident[:, :], compare_op=ALU.not_equal, fill=1.0,
                                        base=0, pattern=[[-1, P]], channel_multiplier=1))
                link(pool.memset(ones[:, :], 1.0))
                link(pool.affine_select(out=tri[:, :], in_=ones[:, :], compare_op=ALU.is_ge, fill=0.0,
                                        base=0, pattern=[[1, P]], channel_multiplier=-1))
                link(pool.iota(iota_n[:, :], pattern=[[1, P]], base=0, channel_multiplier=0,
                               allow_small_or_imprecise_dtypes=True))
                link(pool.iota(iota_e[:, :], pattern=[[1, NE]], base=0, channel_multiplier=0,
                               allow_small_or_imprecise_dtypes=True))
                link(pool.memset(eps[:, :], LN_EPS))
                link(pool.affine_select(out=tile_one[:, :], in_=ones[:, 0:1], compare_op=ALU.is_ge, fill=0.0,
                                        base=-1, pattern=[[0, 1]], channel_multiplier=1))
                link(pool.memset(valid[:, :], 1.0))
                link(pool.affine_select(out=valid[:, NT - 1:NT], in_=ones[:, 0:1], compare_op=ALU.is_ge, fill=0.0,
                                        base=LAST - 1, pattern=[[0, 1]], channel_multiplier=-1))
                link(pool.memset(xres[:, NT - 1, :], 0.0))
                link(pool.memset(idx_ring[:, 0:4], 0))
                link(pool.memset(idx_ring[:, 4:8], 1 << 20))

            @block.sync
            def _(sp):
                sp.dma_start(src_pad[0:E].rearrange("(a b) -> a b", a=16),
                             src.rearrange("(a b) -> a b", a=16)).then_inc(k_pad, 16)
                sp.dma_start(dst_pad[0:E].rearrange("(a b) -> a b", a=16),
                             dst.rearrange("(a b) -> a b", a=16)).then_inc(k_pad, 16)
                for t in range(0, NT - 1, 8):
                    sp.dma_start(xres[:, t:t + 8, :], rows(x, t, t + 8)).then_inc(k_x, 16)
                sp.wait_ge(k_c, 13)
                pad = NBP * EB - E
                rowsp = pad // 4
                done = 0
                while done < rowsp:
                    n = min(P, rowsp - done)
                    lo = E + 4 * done
                    for to, c in ((src_pad, 0), (dst_pad, 4)):
                        sp.dma_start(to[lo:lo + 4 * n].rearrange("(a b) -> a b", b=4),
                                     idx_ring[0:n, c:c + 4]).then_inc(k_pad, 16)
                    done += n
                sp.dma_start(xres[0:LAST, NT - 1, :], x[(NT - 1) * P:N, :]).then_inc(k_x, 16)
                sp.wait_ge(k_pad, 16 * (2 + 2 * math.ceil(rowsp / P)))
                sp.wait_ge(k_x, 16 * ((NT - 1) // 8 + 1))

        q_in, q_c, q_pe, q_g, q_t, q_o, q_v = (sem(n) for n in
            ("q_in", "q_c", "q_pe", "q_g", "q_t", "q_o", "q_v"))
        HB = NBP // 2
        last_i = acc_flat[0:1, 0:NBP].bitcast(I32)
        last_f = acc_flat[0:1, NBP:2 * NBP]
        below = acc_flat[0:P, 2 * NBP:3 * NBP]
        base = 3 * NBP
        tlow = acc_flat[:, base:base + 1]
        tnum = acc_flat[:, base + 1:base + 2]
        pstart = acc_flat[:, base + 2:base + 3]
        piota = acc_flat[:, base + 8:base + 8 + PCOL]
        ind = acc_flat[:, base + 8 + PCOL:base + 8 + 2 * PCOL]
        b2 = base + 8 + 2 * PCOL
        pcol = acc_flat[:, b2:b2 + PCH]
        tcol = acc_flat[:, b2 + 8:b2 + 8 + PCH]
        bcol = acc_flat[:, b2 + 16:b2 + 16 + PCH]
        bidx = acc_flat[:, b2 + 24:b2 + 24 + PCH].bitcast(I32)
        lowcol = acc_flat[:, b2 + 32:b2 + 32 + PCH]
        b3 = b2 + 64
        raw = acc_flat[:, b3:b3 + 2 * PCH * EB].bitcast(I32).rearrange("p (a k e) -> p a k e", a=2, k=PCH)
        b4 = b3 + 2 * PCH * EB
        cooked = acc_flat[:, b4:b4 + 2 * PCH * EB].rearrange("p (a k e) -> p a k e", a=2, k=PCH)
        trow = acc_flat[0:1, b4 + 2 * PCH * EB:b4 + 2 * PCH * EB + PCOL]
        assert b4 + 2 * PCH * EB + PCOL <= NT * AW
        with nc.Block() as block:
            @block.sync
            def _(sp):
                sp.dma_start(last_i.rearrange("a (b c) -> a b c", c=1),
                             dst_pad.rearrange("(a b c) -> a b c", a=1, c=EB)[:, :, EB - 1:EB]).then_inc(q_in, 16)
                sp.wait_ge(q_t, 4 * PCH)
                sp.dma_start(src_cols, src_sb).then_inc(q_o, 16)
                sp.dma_start(dst_cols, dst_sb).then_inc(q_o, 16)
                sp.wait_ge(q_o, 32)

            @block.gpsimd
            def _(pool):
                link = Chain(pool, q_c)
                link(pool.iota(tlow, pattern=[[0, 1]], base=0, channel_multiplier=P,
                               allow_small_or_imprecise_dtypes=True))
                link(pool.iota(tnum, pattern=[[0, 1]], base=0, channel_multiplier=1,
                               allow_small_or_imprecise_dtypes=True))
                link(pool.iota(piota, pattern=[[1, PCOL]], base=0, channel_multiplier=0,
                               allow_small_or_imprecise_dtypes=True))
                link(pool.iota(pcol, pattern=[[P, PCH]], base=0, channel_multiplier=1,
                               allow_small_or_imprecise_dtypes=True))
                pool.wait_ge(q_v, 9)
                for k in range(PCH):
                    for a, table in enumerate((src_pad, dst_pad)):
                        pool.indirect_dma_start(out=raw[:, a, k, :], out_offset=None,
                                                in_=table.rearrange("(b e) -> b e", e=EB),
                                                in_offset=bass.IndirectOffsetOnAxis(ap=bidx[:, k:k + 1], axis=0)
                                                ).then_inc(q_g, 16)

            @block.vector
            def _(dve):
                link = Chain(dve, q_v)
                dve.wait_ge(q_in, 16)
                link(dve.tensor_copy(last_f, last_i))
                dve.wait_ge(q_pe, 1)
                dve.wait_ge(q_c, 4)
                for h in range(2):
                    dve.tensor_scalar(below[:, h * HB:(h + 1) * HB], psum[h][:, 0:HB], tlow, None,
                                      ALU.is_lt).then_inc(q_v, 1)
                dve.wait_ge(q_v, 3)
                link.n = 3
                link(dve.reduce_sum(pstart, below, AX_X))
                link(dve.tensor_tensor(pstart, pstart, tnum, ALU.add))
                link(dve.tensor_scalar(ind, piota, pstart, None, ALU.is_ge))
                dve.wait_ge(q_pe, 2)
                link(dve.tensor_copy(tcol, psum[2][:, 0:PCH]))
                link(dve.tensor_tensor(bcol, pcol, tcol, ALU.subtract))
                link(dve.tensor_scalar(bidx, bcol, float(NBP - 1), None, ALU.min))
                link(dve.tensor_scalar(lowcol, tcol, float(P), None, ALU.mult))
                for h in range(2):
                    link(dve.tensor_copy(trow[:, h * (PCOL // 2):(h + 1) * (PCOL // 2)],
                                         psum[3 + h][0:1, 0:PCOL // 2]))
                four = trow[:, 0:UN * STEPS].rearrange("p (s u) -> p u s", u=UN)
                link(dve.scalar_tensor_tensor(out=below[0:1, 0:STEPS], in0=four[:, 3, :], scalar=64.0,
                                              in1=four[:, 2, :], op0=ALU.mult, op1=ALU.add))
                link(dve.scalar_tensor_tensor(out=below[0:1, 0:STEPS], in0=below[0:1, 0:STEPS], scalar=64.0,
                                              in1=four[:, 1, :], op0=ALU.mult, op1=ALU.add))
                link(dve.scalar_tensor_tensor(out=tpack[0:1, :], in0=below[0:1, 0:STEPS], scalar=64.0,
                                              in1=four[:, 0, :], op0=ALU.mult, op1=ALU.add))
                dve.wait_ge(q_g, 16 * 2 * PCH)
                for k in range(PCH):
                    dve.tensor_copy(cooked[:, 0, k, :], raw[:, 0, k, :]).then_inc(q_v, 1)
                    dve.tensor_scalar(cooked[:, 1, k, :], raw[:, 1, k, :], lowcol[:, k:k + 1], None,
                                      ALU.subtract).then_inc(q_v, 1)
                for k in range(PCH):
                    for a, to in enumerate((src_sb, dst_sb)):
                        for j in range(2):
                            n = (2 * k + a) * 2 + j
                            dve.wait_ge(q_pe, 3 + n)
                            dve.tensor_copy(to.rearrange("p (c j) -> p j c", j=2)[:, j, k * P:(k + 1) * P],
                                            psum[n % 8][:, 0:P]).then_inc(q_t, 1)

            @block.tensor
            def _(pe):
                pe.wait_ge(q_v, 1)
                for h in range(2):
                    last = pe.matmul(psum[h][:, 0:HB], ones[0:1, :], last_f[:, h * HB:(h + 1) * HB],
                                     start=True, stop=True)
                last.then_inc(q_pe, 1)
                pe.wait_ge(q_v, 6)
                for k in range(PCH):
                    pe.matmul(psum[2][:, k:k + 1], ind[0:NT, k * P:(k + 1) * P], tile_one[0:NT, 0:1],
                              start=True, stop=True)
                for h in range(2):
                    last = pe.matmul(psum[3 + h][0:1, 0:PCOL // 2], tile_one[0:NT, 0:1],
                                     ind[0:NT, h * (PCOL // 2):(h + 1) * (PCOL // 2)], start=True, stop=True)
                last.then_inc(q_pe, 1)
                pe.wait_ge(q_v, 15 + 2 * PCH)
                for k in range(PCH):
                    for a in range(2):
                        for j in range(2):
                            n = (2 * k + a) * 2 + j
                            if n >= 8:
                                pe.wait_ge(q_t, n - 7)
                            pe.transpose(psum[n % 8][:, 0:P], cooked[:, a, k, j * P:(j + 1) * P],
                                         ident[:, :]).then_inc(q_pe, 1)

        def row_stats(tag):
            s_st, s_v, s_sq = sem(tag + "_st"), sem(tag + "_v"), sem(tag + "_sq")
            t_a, t_b, var = lnt[:, 3, :], lnt[:, 4, :], lnt[:, 5, :]
            with nc.Block() as block:
                @block.vector
                def _(dve):
                    with dve.Fori(0, NG) as i:
                        for u in range(TB):
                            t = i * TB + u
                            dve.bn_stats(stats[:, bass.ds(t, 1), :], xflat[:, bass.ds(t * D, D)]).then_inc(s_st, 1)
                    dve.wait_ge(s_st, NT)
                    link = Chain(dve, s_v)
                    me, ve, mo, vo = (stats[:, :, c] for c in (1, 2, 4, 5))
                    link(dve.tensor_tensor(t_a, me, mo, ALU.add))
                    link(dve.tensor_scalar(mean, t_a, 0.5, None, ALU.mult))
                    link(dve.tensor_tensor(t_a, me, mo, ALU.subtract))
                    link(dve.scalar_tensor_tensor(out=t_b, in0=t_a, scalar=0.25, in1=t_a, op0=ALU.mult, op1=ALU.mult))
                    link(dve.tensor_tensor(t_a, ve, vo, ALU.add))
                    link(dve.scalar_tensor_tensor(out=var, in0=t_a, scalar=1.0 / D, in1=t_b,
                                                  op0=ALU.mult, op1=ALU.add))
                    dve.wait_ge(s_sq, 1)
                    link(dve.reciprocal(rstd, t_a))
                    link(dve.scalar_tensor_tensor(out=nmr, in0=mean, scalar=-1.0, in1=rstd,
                                                  op0=ALU.mult, op1=ALU.mult))

                @block.scalar
                def _(act):
                    act.wait_ge(s_v, 6)
                    act.activation(t_a, var, ACT.Sqrt, bias=eps[:, 0:1]).then_inc(s_sq, 1)

        def project(tag, width, w_sb, rows_of, evac, load, n_load, before=None, n_before=0, store=None):
            s = {n: sem(tag + "_" + n) for n in ("w", "y", "t", "yt", "f", "e", "b")}
            s["out"] = [sem(f"{tag}_out{u}") for u in range(TB)]
            with nc.Block() as block:
                @block.sync
                def _(sp):
                    load(sp, s["w"])
                    if store:
                        rolled(sp, NG, lambda i: [store(sp, s, i, u) for u in range(TB)])
                        for u in range(TB):
                            sp.wait_ge(s["out"][u], 16 * NG)

                @block.scalar
                def _(act):
                    def body(i):
                        for u in range(TB):
                            if "act" in rows_of:
                                wait(act, s["t"], (i - 1) * TB + u + 1)
                                rows_of["act"](act, s, i * TB + u, u)
                            if "act" in evac and u:
                                evac["act"](act, s, i, u - 1)
                        if "act" in evac:
                            evac["act"](act, s, i, TB - 1)
                    rolled(act, NG, body)

                @block.vector
                def _(dve):
                    if before:
                        before(dve, s)

                    def transposed(i, u):
                        k = i * TB + u
                        dve.wait_ge(s["t"], k + 1)
                        wait(dve, s["f"], k if u == 0 else k - 2)
                        dve.tensor_copy(yt_ring[:, u % 3, :], psum[u % 3][:, 0:D]).then_inc(s["yt"], 1)

                    def body(i):
                        for u in range(TB):
                            if "dve" in rows_of:
                                rows_of["dve"](dve, s, i * TB + u, u)
                            transposed(i, u)
                            if "dve" in evac and u:
                                evac["dve"](dve, s, i, u - 1)
                        if "dve" in evac:
                            evac["dve"](dve, s, i, TB - 1)
                    rolled(dve, NG, body)

                @block.tensor
                def _(pe):
                    pe.wait_ge(s["w"], n_load)
                    wait(pe, s["b"], n_before)

                    def turn(i, u):
                        k = i * TB + u
                        pe.wait_ge(s["y"], k + 1)
                        wait(pe, s["yt"], k if u == 0 else k - 2)
                        for c in range(KC):
                            last = pe.transpose(psum[u % 3][:, c * P:(c + 1) * P],
                                                cols(y_ring[:, u, :], c), ident[:, :])
                        last.then_inc(s["t"], 1)

                    def product(i, u):
                        k = i * TB + u
                        pe.wait_ge(s["yt"], k + 1)
                        wait(pe, s["e"], k if u == 0 else k - 2)
                        for c in range(KC):
                            last = pe.matmul(psum[3 + u % 3][:, 0:width], yt_ring[:, u % 3, c * P:(c + 1) * P],
                                             w_sb[:, c, 0:width], start=(c == 0), stop=(c == KC - 1))
                        last.then_inc(s["f"], 1)

                    def body(i):
                        turn(i, 0)
                        for u in range(1, TB):
                            turn(i, u)
                            product(i, u - 1)
                        product(i, TB - 1)
                    rolled(pe, NG, body)

        def layernorm_rows(act, s, t, u):
            act.activation(y_ring[:, u, :], xflat[:, bass.ds(t * D, D)], ACT.Identity,
                           bias=own(nmr, t), scale=own(rstd, t)).then_inc(s["y"], 1)

        def walk(tag, attention):
            table, gw = (table0, GW) if attention else (table1, D)
            mw = MW if attention else D
            s_in, s_oh, s_t, s_ht, s_b, s_z, s_w, s_m, s_a, s_acc, s_idx, s_c, s_one = (
                sem(tag + "_" + n) for n in ("in", "oh", "t", "ht", "b", "z", "w", "m", "a", "acc", "idx", "c", "one"))
            s_g = [sem(f"{tag}_g{u}") for u in range(UN)]
            s_go, s_zero = sem(tag + "_go"), sem(tag + "_zero")
            zt = small[:, :].rearrange("p (u j h) -> p u j h", u=UN, j=2)
            banks_t = [psum[u % 2][:, 0:EB] for u in range(UN)]
            banks_e = [psum[2 + u % 2][:, 0:16].rearrange("p (j h) -> p j h", j=2) for u in range(UN)]
            banks_a = [psum[4 + u] for u in range(UN)]
            table_row = table

            def gather(pool, u):
                for j in range(2):
                    pool.indirect_dma_start(out=got[:, u, j, 0:gw], out_offset=None, in_=table_row,
                                            in_offset=bass.IndirectOffsetOnAxis(
                                                ap=idx_ring[:, 2 * u + j:2 * u + j + 1], axis=0)
                                            ).then_inc(s_g[u], 16)

            def tiles_of(eng, i):
                word = eng.value_load(tpack[0:1, bass.ds(i, 1)], min_val=0, max_val=(1 << 24) - 1)
                return [eng.snap((word // (1 << (6 * u))) % 64) for u in range(UN)]

            with nc.Block() as block:
                @block.sync
                def _(sp):
                    sp.dma_start(src_sb, src_cols).then_inc(s_in, 16)
                    sp.dma_start(dst_sb, dst_cols).then_inc(s_in, 16)
                    if attention:
                        sp.wait_ge(s_one, 2)
                        for t in range(0, TILES1, TB):
                            n = min(TB, TILES1 - t)
                            sp.dma_start(rows(expert_in, t, t + n), y_ring[:, 0:n, :]).then_inc(s_zero, 16)
                        sp.wait_ge(s_zero, 16 * math.ceil(TILES1 / TB))

                @block.gpsimd
                def _(pool):
                    def step(i, u):
                        pool.wait_ge(s_idx, UN * i + u + 1)
                        wait(pool, s_m if attention else s_a, UN * (i - 1) + u + 1)
                        pool.sem_inc(s_go, 1)
                        gather(pool, u)
                    rolled(pool, STEPS, lambda i: [step(i, u) for u in range(UN)])

                @block.scalar
                def _(act):
                    def stage_idx(i, u):
                        c = 2 * (UN * (i + 1) + u)
                        if not (isinstance(i, int) and i < 0):
                            act.wait_ge(s_g[u], 32 * (i + 1))
                        act.copy(idx_ring[:, 2 * u:2 * u + 2], src_sb[:, bass.ds(c, 2)]).then_inc(s_idx, 1)

                    def copy_onehot(i, u):
                        act.wait_ge(s_t, UN * i + u + 1)
                        act.copy(onehot_t[:, u, :, :].rearrange("p j n -> p (j n)"), banks_t[u]).then_inc(s_ht, 1)

                    def weights(i, u):
                        act.wait_ge(s_z, UN * i + u + 1)
                        act.activation(msg[:, u, :, D:GW], zt[:, u, :, 4:8], ACT.Exp).then_inc(s_w, 1)

                    act.wait_ge(s_in, 32)
                    for u in range(UN):
                        stage_idx(-1, u)
                    if attention:
                        for u in range(UN):
                            copy_onehot(0, u)

                    def body(i):
                        for u in range(UN):
                            if attention:
                                weights(i, u)
                            stage_idx(i, u)
                        if attention:
                            for u in range(UN):
                                copy_onehot(i + 1, u)
                    rolled(act, STEPS, body)

                @block.vector
                def _(dve):
                    def make_onehot(i, u):
                        c = 2 * (UN * i + u)
                        dve.tensor_tensor(onehot[:, u, :, :], iota_n[:, :].unsqueeze(1).broadcast_to([P, 2, P]),
                                          dst_sb[:, bass.ds(c, 2)].unsqueeze(2).broadcast_to([P, 2, P]),
                                          ALU.is_equal).then_inc(s_oh, 1)

                    def scores(i, u):
                        n = UN * i + u
                        z, zz = zt[:, u, :, 0:4], zt[:, u, :, 4:8]
                        dve.wait_ge(s_b, n + 1)
                        dve.wait_ge(s_g[u], 32 * (i + 1))
                        dve.tensor_tensor(z, got[:, u, :, D:GW], banks_e[u][:, :, 0:4], ALU.add).then_inc(s_c, 1)
                        dve.wait_ge(s_c, 3 * n + 1)
                        dve.scalar_tensor_tensor(out=zz, in0=z, scalar=0.2, in1=z, op0=ALU.mult,
                                                 op1=ALU.max).then_inc(s_c, 1)
                        dve.wait_ge(s_c, 3 * n + 2)
                        dve.tensor_tensor(z, zz, banks_e[u][:, :, 4:8], ALU.subtract).then_inc(s_c, 1)
                        dve.wait_ge(s_c, 3 * n + 3)
                        dve.tensor_scalar(zz, z, 0.0, None, ALU.min).then_inc(s_z, 1)

                    def messages(i, u):
                        dve.wait_ge(s_w, UN * i + u + 1)
                        for j in range(2):
                            last = dve.tensor_tensor(
                                msg[:, u, j, 0:D].rearrange("p (h d) -> p h d", h=HEADS),
                                got[:, u, j, 0:D].rearrange("p (h d) -> p h d", h=HEADS),
                                msg[:, u, j, D:GW].unsqueeze(2).broadcast_to([P, HEADS, HD]), ALU.mult)
                        last.then_inc(s_m, 1)

                    def collect(i, u, t):
                        n = UN * i + u
                        dve.wait_ge(s_a, n + 1)
                        wait(dve, s_acc, n)
                        cell = arena[:, bass.ds(t * AW, mw)]
                        dve.tensor_tensor(cell, cell, banks_a[u][:, 0:mw], ALU.add).then_inc(s_acc, 1)

                    if attention:
                        dve.memset(msg[:, :, :, GW:AW], 1.0).then_inc(s_one, 1)
                        dve.memset(y_ring, 0.0).then_inc(s_one, 1)
                    dve.wait_ge(s_in, 32)
                    for u in range(UN):
                        make_onehot(0, u)

                    def body(i):
                        tiles = tiles_of(dve, i)
                        if attention:
                            scores(i, 0)
                            scores(i, 1)
                            messages(i, 0)
                            scores(i, 2)
                            messages(i, 1)
                            collect(i, 0, tiles[0])
                            make_onehot(i + 1, 0)
                            scores(i, 3)
                            messages(i, 2)
                            collect(i, 1, tiles[1])
                            make_onehot(i + 1, 1)
                            messages(i, 3)
                            for u in (2, 3):
                                collect(i, u, tiles[u])
                                make_onehot(i + 1, u)
                        else:
                            for u in range(UN):
                                collect(i, u, tiles[u])
                                make_onehot(i + 1, u)
                    rolled(dve, STEPS, body)

                @block.tensor
                def _(pe):
                    def turn(i, u):
                        pe.wait_ge(s_oh, UN * i + u + 1)
                        wait(pe, s_ht, UN * i + u - 1)
                        for j in range(2):
                            last = pe.transpose(banks_t[u][:, j * P:(j + 1) * P], onehot[:, u, j, :], ident[:, :])
                        last.then_inc(s_t, 1)

                    def spread(i, u, t):
                        pe.wait_ge(s_ht, UN * i + u + 1)
                        wait(pe, s_z, UN * i + u - 1)
                        for j in range(2):
                            last = pe.matmul(banks_e[u][:, j, :], onehot_t[:, u, j, :],
                                             arena[:, bass.ds(t * 8 + er_at, 8)],
                                             start=True, stop=True)
                        last.then_inc(s_b, 1)

                    def add_up(i, u):
                        n = UN * i + u
                        if attention:
                            pe.wait_ge(s_m, n + 1)
                        else:
                            pe.wait_ge(s_oh, n + 1)
                            pe.wait_ge(s_g[u], 32 * (i + 1))
                        wait(pe, s_acc, UN * (i - 1) + u + 1)
                        for j in range(2):
                            last = pe.matmul(banks_a[u][:, 0:mw], onehot[:, u, j, :],
                                             (msg if attention else got)[:, u, j, 0:mw],
                                             start=(j == 0), stop=(j == 1))
                        last.then_inc(s_a, 1)

                    if attention:
                        pe.wait_ge(s_one, 1)
                        for u in range(UN):
                            turn(0, u)

                        def body(i):
                            tiles = tiles_of(pe, i)
                            for u in range(3):
                                spread(i, u, tiles[u])
                            add_up(i, 0)
                            spread(i, 3, tiles[3])
                            add_up(i, 1)
                            turn(i + 1, 0)
                            add_up(i, 2)
                            turn(i + 1, 1)
                            add_up(i, 3)
                            turn(i + 1, 2)
                            turn(i + 1, 3)
                        rolled(pe, STEPS, body)
                    else:
                        rolled(pe, STEPS, lambda i: [add_up(i, u) for u in range(UN)])

        row_stats("ln0")

        def load_gat(sp, s):
            sp.dma_start(wraw, g0_w.rearrange("(c k) n -> k c n", c=KC)).then_inc(s, 16)
            for a, v in enumerate((g0_al, g0_ar)):
                sp.dma_start(attn[:, a, :], v.rearrange("h d -> (h d)").partition_broadcast(P)).then_inc(s, 16)

        def build_gat(dve, s):
            dve.wait_ge(s["w"], 48)
            link = Chain(dve, s["b"])
            link(dve.tensor_copy(wproj[:, :, 0:D], wraw))
            for c in range(KC):
                for a in range(2):
                    link(dve.tensor_tensor(stage_flat[:, 0:D], wraw[:, c, :], attn[:, a, :], ALU.mult))
                    link(dve.reduce_sum(wproj[:, c, D + HEADS * a:D + HEADS * (a + 1)],
                                        stage_flat[:, 0:D].rearrange("p (h d) -> p h d", h=HEADS), AX_X))

        def add_h(dve, s, t, u):
            dve.wait_ge(s["y"], t + 1)
            xs = xflat[:, bass.ds(t * D, D)]
            dve.tensor_tensor(xs, xs, y_ring[:, u, :], ALU.add).then_inc(s["b"], 1)

        def gat_out_act(act, s, i, u):
            k = i * TB + u
            act.wait_ge(s["f"], k + 1)
            wait(act, s["out"][u], 16 * i)
            act.copy(stage[:, u, :], psum[3 + u % 3][:, 0:AW]).then_inc(s["e"], 1)

        def gat_out_dve(dve, s, i, u):
            k = i * TB + u
            dve.wait_ge(s["e"], k + 1)
            dve.tensor_copy(el_flat[:, bass.ds(k * HEADS, HEADS)], stage[:, u, D:GW]).then_inc(s["b"], 1)
            dve.tensor_copy(er_flat[:, bass.ds(k * 8, HEADS)], stage[:, u, GW:AW]).then_inc(s["b"], 1)

        def gat_store(sp, s, i, u):
            k = i * TB + u
            sp.wait_ge(s["e"], k + 1)
            sp.dma_start(table0[bass.ds(k * P, P), :], stage[:, u, 0:GW]).then_inc(s["out"][u], 16)

        el_flat = el_all.rearrange("p t n -> p (t n)")
        er_flat = er_u.rearrange("p t n -> p (t n)")

        def layernorm_after(act, s, t, u):
            wait(act, s["b"], 9 + 3 * t - 3 * (TB - 1))
            layernorm_rows(act, s, t, u)

        project("gat", AW, wproj, {"act": layernorm_rows, "dve": add_h},
                {"act": gat_out_act, "dve": gat_out_dve}, load_gat, 48, before=build_gat, n_before=9,
                store=gat_store)

        m_v, m_p = sem("m_v"), sem("m_p")
        with nc.Block() as block:
            @block.gpsimd
            def _(pool):
                pool.memset(acc_flat, 0.0).then_inc(m_p, 1)
                pool.wait_ge(m_v, 1)
                pool.partition_all_reduce(small[:, 4:8], small[:, 0:4], P, RMAX).then_inc(m_p, 1)
                pool.wait_ge(m_p, 2)

            @block.vector
            def _(dve):
                link = Chain(dve, m_v)
                link(dve.tensor_reduce(small[:, 0:4], el_all.rearrange("p t n -> p n t"), AX_X, ALU.max))
                dve.wait_ge(m_p, 2)
                er, bound = er_u[:, :, 0:4], er_u[:, :, 4:8]
                link(dve.tensor_tensor(el_all, er, small[:, 4:8].unsqueeze(1).broadcast_to([P, NT, HEADS]), ALU.add))
                link(dve.scalar_tensor_tensor(out=bound, in0=el_all, scalar=0.2, in1=el_all,
                                              op0=ALU.mult, op1=ALU.max))

        walk("gat_walk", True)

        a_v, a_s, a_in = sem("a_v"), sem("a_s"), sem("a_in")
        with nc.Block() as block:
            @block.sync
            def _(sp):
                sp.dma_start(bias_bc, g0_bias.partition_broadcast(P)).then_inc(a_in, 16)
                sp.dma_start(gate_w[:, :, :], f0_gw.rearrange("(c k) n -> k c n", c=KC)).then_inc(a_in, 16)
                sp.dma_start(gate_b[:, :], f0_gb.partition_broadcast(P)).then_inc(a_in, 16)
                sp.wait_ge(a_in, 48)

            @block.vector
            def _(dve):
                link = Chain(dve, a_v)
                den = acc[:, :, D:GW]
                link(dve.tensor_scalar(den, den, 1e-30, None, ALU.max))
                link(dve.reciprocal(den, den))
                link(dve.tensor_scalar(lnt[:, 3, :], acc[:, :, GW], 1.0, None, ALU.add))
                dve.wait_ge(a_s, 1)
                link(dve.reciprocal(dis[:, :], lnt[:, 4, :]))
                dve.wait_ge(a_in, 48)
                for g in range(NG):
                    t0, t1 = g * TB, (g + 1) * TB
                    a = acc[:, t0:t1, 0:D]
                    for t in range(t0, t1):
                        ah = acc[:, t, 0:D].rearrange("p (h d) -> p h d", h=HEADS)
                        dve.tensor_tensor(ah, ah, acc[:, t, D:GW].unsqueeze(2).broadcast_to([P, HEADS, HD]),
                                          ALU.mult).then_inc(a_v, 1)
                    link.n += TB
                    dve.wait_ge(a_v, link.n)
                    link(dve.tensor_tensor(a, a, bias_bc.unsqueeze(1).broadcast_to([P, TB, D]), ALU.add))
                    link(dve.tensor_scalar(stage[:, :, 0:D], a, 0.0, None, ALU.min))
                    dve.wait_ge(a_s, 2 + g)
                    link(dve.scalar_tensor_tensor(out=a, in0=a, scalar=0.0, in1=stage[:, :, 0:D],
                                                  op0=ALU.max, op1=ALU.add))
                    link(dve.scalar_tensor_tensor(out=xres[:, t0:t1, :], in0=a, scalar=-1.0,
                                                  in1=xres[:, t0:t1, :], op0=ALU.add, op1=ALU.add))

            @block.scalar
            def _(act):
                act.wait_ge(a_v, 3)
                act.activation(lnt[:, 4, :], lnt[:, 3, :], ACT.Sqrt).then_inc(a_s, 1)
                for g in range(NG):
                    act.wait_ge(a_v, 4 + g * (TB + 4) + TB + 2)
                    act.activation(stage[:, :, 0:D], stage[:, :, 0:D], ACT.Exp).then_inc(a_s, 1)


        def load_gate(w, b):
            def load(sp, s):
                sp.dma_start(gate_w[:, :, :], w.rearrange("(c k) n -> k c n", c=KC)).then_inc(s, 16)
                sp.dma_start(gate_b[:, :], b.partition_broadcast(P)).then_inc(s, 16)
            return load

        def take_logits(dve, s, i, u):
            k = i * TB + u
            dve.wait_ge(s["f"], k + 1)
            dve.tensor_tensor(logit[:, :, :].rearrange("p t e -> p (t e)")[:, bass.ds(k * NE, NE)],
                              psum[3 + u % 3][:, 0:NE], gate_b[:, :], ALU.add).then_inc(s["e"], 1)

        def route(tag, choices, cap):
            s_v, s_a, s_p = sem(tag + "_v"), sem(tag + "_a"), sem(tag + "_p")
            W = NT * NE
            at = [0]

            def tmp(width):
                at[0] += width
                return arena[:, at[0] - width:at[0]]

            def grid():
                return tmp(W).rearrange("p (t e) -> p t e", e=NE)

            probs, hit, chosen, tot, incl, place, within, t0 = (grid() for _ in range(8))
            oh = [grid() for _ in range(choices)]
            top = [tmp(NT) for _ in range(choices)]
            red, red2, m = tmp(NT), tmp(NT), tmp(NT)
            num, tiles_of_e, ends, start, rowbase, iota_m = (tmp(NE) for _ in range(6))
            num_i = tmp(NE).bitcast(I32)
            te = tmp(P)

            def over_e(a):
                return a.unsqueeze(2).broadcast_to([P, NT, NE])

            def over_t(a):
                return a.unsqueeze(1).broadcast_to([P, NT, NE])

            with nc.Block() as block:
                @block.scalar
                def _(act):
                    act.wait_ge(s_v, 2)
                    act.activation(probs, probs, ACT.Exp).then_inc(s_a, 1)

                @block.tensor
                def _(pe):
                    pe.wait_ge(s_p, 1)
                    flat = chosen.rearrange("p t e -> p (t e)")
                    pe.matmul(psum[0][:, 0:W], tri[:, :], flat, start=True, stop=True)
                    pe.matmul(psum[1][:, 0:W], ones[:, :], flat, start=True, stop=True).then_inc(s_p, 1)

                @block.vector
                def _(dve):
                    link = Chain(dve, s_v)
                    link(dve.tensor_reduce(red, logit[:, :, :], AX_X, ALU.max))
                    link(dve.tensor_tensor(probs, logit[:, :, :], over_e(red), ALU.subtract))
                    dve.wait_ge(s_a, 1)
                    link(dve.reduce_sum(red, probs, AX_X))
                    link(dve.reciprocal(red2, red))
                    link(dve.tensor_tensor(probs, probs, over_e(red2), ALU.mult))
                    link(dve.tensor_scalar(iota_m, iota_e[:, :], -float(NE), None, ALU.add))
                    for k in range(choices):
                        link(dve.tensor_reduce(top[k], probs, AX_X, ALU.max))
                        link(dve.tensor_tensor(hit, probs, over_e(top[k]), ALU.is_equal))
                        link(dve.tensor_tensor(hit, hit, over_t(iota_m), ALU.mult))
                        link(dve.tensor_reduce(red, hit, AX_X, ALU.min))
                        link(dve.tensor_tensor(oh[k], over_t(iota_m), over_e(red), ALU.is_equal))
                        if k + 1 < choices:
                            link(dve.scalar_tensor_tensor(out=probs, in0=oh[k], scalar=-4.0, in1=probs,
                                                          op0=ALU.mult, op1=ALU.add))
                        link(dve.tensor_tensor(oh[k], oh[k], over_e(valid[:, :]), ALU.mult))
                    if choices == 1:
                        link(dve.tensor_copy(chosen, oh[0]))
                    else:
                        link(dve.tensor_tensor(chosen, oh[0], oh[1], ALU.add))
                    dve.sem_inc(s_p, 1)
                    dve.wait_ge(s_p, 2)
                    link(dve.tensor_copy(tot, psum[1][:, 0:W].rearrange("p (t e) -> p t e", e=NE)))
                    for e in range(NE):
                        link(dve.tensor_tensor_scan(incl[:, :, e], ones[:, 0:NT], tot[:, :, e], 0.0,
                                                    ALU.mult, ALU.add))
                    link(dve.tensor_tensor(place, incl, tot, ALU.subtract))
                    link(dve.scalar_tensor_tensor(out=place, in0=psum[0][:, 0:W].rearrange("p (t e) -> p t e", e=NE),
                                                  scalar=-1.0, in1=place, op0=ALU.add, op1=ALU.add))
                    link(dve.tensor_scalar(within, place, float(cap), None, ALU.is_lt))
                    link(dve.tensor_scalar(num, incl[:, NT - 1, :], float(cap), float(P - 1), ALU.min, ALU.add))
                    link(dve.tensor_copy(num_i, num))
                    link(dve.tensor_scalar(num_i, num_i, 7, None, ALU.arith_shift_right))
                    link(dve.tensor_copy(tiles_of_e, num_i))
                    link(dve.tensor_tensor_scan(ends, ones[:, 0:NE], tiles_of_e, 0.0, ALU.mult, ALU.add))
                    link(dve.tensor_tensor(start, ends, tiles_of_e, ALU.subtract))
                    link(dve.tensor_scalar(rowbase, start, float(P), None, ALU.mult))
                    link(dve.tensor_tensor(place, place, over_t(rowbase), ALU.add))
                    for k in range(choices):
                        link(dve.tensor_tensor(t0, oh[k], within, ALU.mult))
                        link(dve.reduce_sum(m, t0, AX_X))
                        link(dve.tensor_tensor(t0, t0, place, ALU.mult))
                        link(dve.reduce_sum(red, t0, AX_X))
                        link(dve.tensor_copy(slot[:, 2 * k + 1, :], red))
                        link(dve.tensor_scalar(red2, m, -float(1 << 20), float(1 << 20), ALU.mult, ALU.add))
                        link(dve.tensor_tensor(slot[:, 2 * k, :], red, red2, ALU.add))
                        if choices == 1:
                            link(dve.tensor_tensor(wgt[:, 0, :], top[0], m, ALU.mult))
                    if choices == 2:
                        link(dve.tensor_tensor(red, top[0], top[1], ALU.add))
                        link(dve.reciprocal(red2, red))
                        for k in range(2):
                            link(dve.tensor_tensor(wgt[:, k, :], top[k], red2, ALU.mult))
                    link(dve.tensor_scalar(te, iota_n[:, :], start[:, 1:2], None, ALU.is_ge))
                    for e in range(2, NE):
                        link(dve.scalar_tensor_tensor(out=te, in0=iota_n[:, :], scalar=start[:, e:e + 1], in1=te,
                                                      op0=ALU.is_ge, op1=ALU.add))
                    link(dve.tensor_copy(tile_e[:, :], te[0:1, :]))

        def dispatch(tag, choices, tiles):
            s_go = sem(tag + "_go")
            s_out = [sem(f"{tag}_s{u}") for u in range(TB)]
            with nc.Block() as block:
                @block.scalar
                def _(act):
                    with act.Fori(0, NT) as t:
                        act.activation(y_all[:, bass.ds(t * D, D)], xflat[:, bass.ds(t * D, D)], ACT.Identity,
                                       bias=own(nmr, t), scale=own(rstd, t)).then_inc(s_go, 1)

                @block.gpsimd
                def _(pool):
                    for t in range(NT):
                        pool.wait_ge(s_go, t + 1)
                        wait(pool, s_out[t % TB], 16 * choices * (t // TB))
                        for k in range(choices):
                            pool.indirect_dma_start(
                                out=expert_in, out_offset=bass.IndirectOffsetOnAxis(
                                    ap=slot[:, 2 * k, t:t + 1], axis=0),
                                in_=y_all[:, t * D:(t + 1) * D], in_offset=None,
                                bounds_check=tiles * P - 1, oob_is_err=False).then_inc(s_out[t % TB], 16)
                    for u in range(TB):
                        pool.wait_ge(s_out[u], 16 * choices * NG)

        def experts(tag, tiles, w1, b1, w2, b2, func, affine):
            s_w, s_b, s_bt, s_t, s_x, s_h, s_hm, s_y, s_yo = (
                sem(tag + "_" + n) for n in ("w", "b", "bt", "t", "x", "h", "hm", "y", "yo"))
            s_in = [sem(f"{tag}_in{u}") for u in range(2)]
            s_w1 = [sem(f"{tag}_w1{u}") for u in range(2)]
            w1_rows = w1.rearrange("e k f -> (e k) f")
            s_out = [sem(f"{tag}_out{u}") for u in range(2)]
            raw = y_out.rearrange("p s d -> p (s d)")
            n_raw = 3 if affine else 1
            half = tiles // 2

            def steps(eng, body):
                body(0)
                with eng.Fori(1, half - 1) as i:
                    body(i)
                body(half - 1)

            def first(k):
                return isinstance(k, int) and k == 0

            def last_(k):
                return isinstance(k, int) and k == tiles - 1

            with nc.Block() as block:
                @block.sync
                def _(sp):
                    sp.dma_start(raw[0:NE * FC, 0:P], b1.rearrange("e (c k) -> (e c) k", k=P)).then_inc(s_b, 16)
                    if affine:
                        for a, v in enumerate(affine):
                            sp.dma_start(raw[0:NE * KC, P * (a + 1):P * (a + 2)],
                                         v.rearrange("e (c k) -> (e c) k", k=P)).then_inc(s_b, 16)
                    sp.dma_start(b2_bc, b2.rearrange("e d -> (e d)").partition_broadcast(P)).then_inc(s_w, 16)

                    def load(k, u):
                        wait(sp, s_t, k - 1)
                        sp.dma_start(x_in[:, u, :], expert_in[bass.ds(k * P, P), :]).then_inc(s_in[u], 16)

                    def store(k, u):
                        sp.wait_ge(s_yo, k + 1)
                        sp.dma_start(expert_out[bass.ds(k * P, P), :], y_out[:, u, :]).then_inc(s_out[u], 16)

                    def load_w1(k, u):
                        e = sp.value_load(tile_e[0:1, bass.ds(k, 1)], min_val=0, max_val=NE - 1)
                        wait(sp, s_h, 2 * (k - 1))
                        sp.dma_start(w1_ring[:, u, :, :],
                                     w1_rows[bass.ds(e * D, D), :].rearrange("(c k) f -> k c f", c=KC)
                                     ).then_inc(s_w1[u], 16)

                    for u in range(2):
                        load(u, u)
                        load_w1(u, u)
                    for e in range(NE):
                        sp.dma_start(w2_sb[:, e, :, :], w2[e].rearrange("(c k) d -> k c d", c=FC)).then_inc(s_w, 16)

                    def body(i):
                        for u in range(2):
                            k = 2 * i + u
                            if not (isinstance(k, int) and k + 2 >= tiles):
                                load(k + 2, u)
                                load_w1(k + 2, u)
                            store(k, u)
                    steps(sp, body)
                    for u in range(2):
                        sp.wait_ge(s_out[u], 16 * half)

                @block.vector
                def _(dve):
                    dve.wait_ge(s_w, 16 * (NE + 1))
                    dve.wait_ge(s_bt, 1)
                    dve.tensor_copy(b1_sb[:, :, :].rearrange("p e c -> p (e c)"), psum[0][:, 0:NE * FC]).then_inc(s_bt, 1)
                    if affine:
                        for a, v in enumerate((lg_sb, lb_sb)):
                            dve.tensor_copy(v[:, :, :].rearrange("p e c -> p (e c)"),
                                            psum[1 + a][:, 0:NE * KC]).then_inc(s_bt, 1)
                        dve.wait_ge(s_bt, 4)

                    def rows_in(k, u):
                        dve.wait_ge(s_t, k + 1)
                        wait(dve, s_h, 2 * (k - 1))
                        if affine:
                            e = dve.value_load(tile_e[0:1, bass.ds(k, 1)], min_val=0, max_val=NE - 1)
                            for c in range(KC):
                                last = dve.tensor_scalar(
                                    cols(yt_ring[:, u, :], c), cols(psum[4 + u], c),
                                    lg_sb[:, :, :].rearrange("p e c -> p (e c)")[:, bass.ds(e * KC + c, 1)],
                                    lb_sb[:, :, :].rearrange("p e c -> p (e c)")[:, bass.ds(e * KC + c, 1)],
                                    ALU.mult, ALU.add)
                        else:
                            last = dve.tensor_copy(yt_ring[:, u, :], psum[4 + u][:, 0:D])
                        last.then_inc(s_x, 1)

                    def rows_out(k, u):
                        dve.wait_ge(s_y, k + 1)
                        wait(dve, s_out[u], 8 * (k - u))
                        e = dve.value_load(tile_e[0:1, bass.ds(k, 1)], min_val=0, max_val=NE - 1)
                        dve.tensor_tensor(y_out[:, u, :], psum[6 + u][:, 0:D],
                                          arena[:, bass.ds(e * D + W2W + 2 * KC * FF, D)], ALU.add).then_inc(s_yo, 1)

                    rows_in(0, 0)

                    def body(i):
                        for u in range(2):
                            k = 2 * i + u
                            if not last_(k):
                                rows_in(k + 1, 1 - u)
                            if not first(k):
                                rows_out(k - 1, 1 - u)
                    steps(dve, body)
                    rows_out(tiles - 1, 1)

                @block.scalar
                def _(act):
                    act.wait_ge(s_bt, 2)

                    def body(i):
                        for u in range(2):
                            k = 2 * i + u
                            e = act.value_load(tile_e[0:1, bass.ds(k, 1)], min_val=0, max_val=NE - 1)
                            wait(act, s_y, k - 1)
                            for h in range(2):
                                act.wait_ge(s_h, 2 * k + h + 1)
                                for c in range(h * FC // 2, (h + 1) * FC // 2):
                                    last = act.activation(
                                        hmid[:, u, c, :], psum[2 * u + h][:, (c % 4) * P:(c % 4 + 1) * P], func,
                                        bias=b1_sb[:, :, :].rearrange("p e c -> p (e c)")[:, bass.ds(e * FC + c, 1)])
                                last.then_inc(s_hm, 1)
                    steps(act, body)

                @block.tensor
                def _(pe):
                    pe.wait_ge(s_b, 16 * n_raw)
                    last = pe.transpose(psum[0][:, 0:NE * FC], raw[0:NE * FC, 0:P], ident[0:NE * FC, 0:NE * FC])
                    for a in range(n_raw - 1):
                        last = pe.transpose(psum[1 + a][:, 0:NE * KC], raw[0:NE * KC, P * (a + 1):P * (a + 2)],
                                            ident[0:NE * KC, 0:NE * KC])
                    last.then_inc(s_bt, 1)
                    pe.wait_ge(s_bt, 1 + n_raw)
                    pe.wait_ge(s_w, 16 * (NE + 1))

                    def turn(k, u):
                        pe.wait_ge(s_in[u], 8 * (k - u) + 16)
                        wait(pe, s_x, k - 1)
                        for c in range(KC):
                            last = pe.transpose(cols(psum[4 + u], c), cols(x_in[:, u, :], c), ident[:, :])
                        last.then_inc(s_t, 1)

                    def layer1(k, u):
                        pe.wait_ge(s_x, k + 1)
                        pe.wait_ge(s_w1[u], 8 * (k - u) + 16)
                        for h in range(2):
                            wait(pe, s_hm, 2 * (k - 2) + h + 1)
                            for f in range(h * FC // 2, (h + 1) * FC // 2):
                                for c in range(KC):
                                    last = pe.matmul(psum[2 * u + h][:, (f % 4) * P:(f % 4 + 1) * P],
                                                     w1_ring[:, u, c, f * P:(f + 1) * P],
                                                     cols(yt_ring[:, u, :], c),
                                                     start=(c == 0), stop=(c == KC - 1))
                            last.then_inc(s_h, 1)

                    def layer2(k, u, e):
                        pe.wait_ge(s_hm, 2 * k + 2)
                        wait(pe, s_yo, k - 1)
                        for f in range(FC):
                            last = pe.matmul(psum[6 + u][:, 0:D], hmid[:, u, f, :],
                                             arena[:, bass.ds(e * FC * D + f * D, D)],
                                             start=(f == 0), stop=(f == FC - 1))
                        last.then_inc(s_y, 1)

                    turn(0, 0)

                    def expert(k):
                        return pe.value_load(tile_e[0:1, bass.ds(k, 1)], min_val=0, max_val=NE - 1)

                    def body(i):
                        for u in range(2):
                            k = 2 * i + u
                            layer1(k, u)
                            if not last_(k):
                                turn(k + 1, 1 - u)
                            if not first(k):
                                layer2(k - 1, 1 - u, expert(k - 1))
                    steps(pe, body)
                    layer2(tiles - 1, 1, expert(tiles - 1))

        def combine(tag, choices, tiles, write_out):
            s_v, s_one, s_done, s_out, s_k = (sem(tag + "_" + n) for n in ("v", "one", "done", "out", "k"))
            s_g = [sem(f"{tag}_g{u}") for u in range(TB)]
            picks = [pick_a, pick_b][:choices]
            with nc.Block() as block:
                @block.gpsimd
                def _(pool):
                    for t in range(NT):
                        wait(pool, s_g[t % TB], 16 * choices * (t // TB))
                        for k in range(choices):
                            pool.indirect_dma_start(
                                out=picks[k][:, t, :], out_offset=None, in_=expert_out[0:tiles * P, :],
                                in_offset=bass.IndirectOffsetOnAxis(ap=slot[:, 2 * k + 1, t:t + 1], axis=0)
                                ).then_inc(s_g[t % TB], 16)

                @block.vector
                def _(dve):
                    if choices == 1:
                        zero, high, low = (arena[:, clean_at + c:clean_at + c + 1] for c in range(3))
                        mask = arena[:, clean_at + 8:clean_at + 8 + TB * D].bitcast(I32)
                        link = Chain(dve, s_v)
                        link(dve.memset(zero, 0.0))
                        link(dve.memset(high, 1.0e4))
                        link(dve.memset(low, -1.0e4))
                        for g in range(NG):
                            for u in range(TB):
                                t = g * TB + u
                                dve.wait_ge(s_g[u], 16 * (g + 1))
                                dve.tensor_scalar(pick_a[:, t, :], pick_a[:, t, :], wgt[:, 0, t:t + 1], None,
                                                  ALU.mult).then_inc(s_v, 1)
                            link.n += TB
                            dve.wait_ge(s_v, link.n)
                            y = arena[:, g * TB * D:(g + 1) * TB * D]
                            link(dve.tensor_tensor(mask, y, y, ALU.not_equal))
                            link(dve.copy_predicated(y, mask, zero.broadcast_to([P, TB * D])))
                            link(dve.tensor_scalar(mask, y, FMAX, None, ALU.is_gt))
                            link(dve.copy_predicated(y, mask, high.broadcast_to([P, TB * D])))
                            link(dve.tensor_scalar(mask, y, -FMAX, None, ALU.is_lt))
                            link(dve.copy_predicated(y, mask, low.broadcast_to([P, TB * D])))
                            xs = xflat[:, g * TB * D:(g + 1) * TB * D]
                            link(dve.tensor_tensor(xs, xs, y, ALU.add))
                    else:
                        def body(i):
                            for u in range(TB):
                                t = i * TB + u
                                a, b = (arena[:, bass.ds(t * D + k * NT * D, D)] for k in range(2))
                                xs = xflat[:, bass.ds(t * D, D)]
                                dve.wait_ge(s_g[u], 32 * (i + 1))
                                dve.tensor_scalar(a, a, own(wgt[:, 0, :], t), None, ALU.mult).then_inc(s_v, 1)
                                dve.wait_ge(s_v, 2 * t + 1)
                                dve.scalar_tensor_tensor(out=b, in0=b, scalar=own(wgt[:, 1, :], t), in1=a,
                                                         op0=ALU.mult, op1=ALU.add).then_inc(s_v, 1)
                                dve.wait_ge(s_v, 2 * t + 2)
                                dve.tensor_tensor(xs, xs, b, ALU.add).then_inc(s_done, 1)
                        rolled(dve, NG, body)

                @block.sync
                def _(sp):
                    if write_out:
                        for g in range(NG):
                            sp.wait_ge(s_done, (g + 1) * TB)
                            hi = min((g + 1) * TB, NT - 1)
                            sp.dma_start(rows(out, g * TB, hi), xres[:, g * TB:hi, :]).then_inc(s_out, 16)
                        sp.dma_start(out[(NT - 1) * P:N, :], xres[0:LAST, NT - 1, :]).then_inc(s_out, 16)
                        sp.wait_ge(s_out, 16 * (NG + 1))

        def load_w(w):
            def load(sp, s):
                sp.dma_start(wproj[:, :, 0:D], w.rearrange("(c k) n -> k c n", c=KC)).then_inc(s, 16)
            return load

        def gcn_out(act, s, i, u):
            k = i * TB + u
            act.wait_ge(s["f"], k + 1)
            act.activation(arena[:, bass.ds(k * AW, D)], psum[3 + u % 3][:, 0:D], ACT.Copy,
                           scale=own(dis[:, :], k)).then_inc(s["e"], 1)

        def gcn_store(sp, s, i, u):
            k = i * TB + u
            sp.wait_ge(s["e"], k + 1)
            sp.dma_start(table1[bass.ds(k * P, P), :], arena[:, bass.ds(k * AW, D)]).then_inc(s["out"][u], 16)

        def batchnorm_rows(dve, s, t, u):
            wait(dve, s["t"], t - TB + 1)
            dve.tensor_tensor(y_ring[:, u, :], arena[:, bass.ds(t * AW, D)], bn_g, ALU.mult).then_inc(s["b"], 1)
            dve.wait_ge(s["b"], t + 1)
            dve.tensor_tensor(y_ring[:, u, :], y_ring[:, u, :], bn_b, ALU.add).then_inc(s["y"], 1)

        def batch_stats(tag, b, g, bt, add_to_x):
            s_in, s_z, s_r, s_m, s_v, s_sq, s_c = (sem(tag + "_" + n) for n in ("in", "z", "r", "m", "v", "sq", "c"))
            mu = stage[:, 0, 0:D]

            def group(i):
                return arena[:, bass.ds(i * TB * AW, TB * AW)].rearrange("p (t d) -> p t d", t=TB)[:, :, 0:D]

            def column_sums(pe, bank, source, ready, count):
                for g_ in range(NG):
                    pe.wait_ge(ready, count(g_))
                    for u in range(TB):
                        t = g_ * TB + u
                        r = LAST if t == NT - 1 else P
                        last = pe.matmul(psum[bank][:, 0:D], ones[0:r, :], source(t, u)[0:r, :],
                                         start=(t == 0), stop=(t == NT - 1))
                    last.then_inc(s_m, 1)

            with nc.Block() as block:
                @block.sync
                def _(sp):
                    sp.dma_start(bias_bc, b.partition_broadcast(P)).then_inc(s_in, 16)
                    sp.dma_start(bn_g, g.partition_broadcast(P)).then_inc(s_in, 16)
                    sp.dma_start(bn_b, bt.partition_broadcast(P)).then_inc(s_in, 16)

                @block.vector
                def _(dve):
                    dve.wait_ge(s_in, 48)
                    with dve.Fori(0, NG) as i:
                        for u in range(TB):
                            t = i * TB + u
                            a = arena[:, bass.ds(t * AW, D)]
                            dve.scalar_tensor_tensor(out=a, in0=a, scalar=own(dis[:, :], t), in1=bias_bc,
                                                     op0=ALU.mult, op1=ALU.add).then_inc(s_z, 1)
                    dve.wait_ge(s_m, NG)
                    link = Chain(dve, s_v)
                    link(dve.tensor_scalar(mu, psum[0][:, 0:D], 1.0 / N, None, ALU.mult))
                    with dve.Fori(0, NG) as i:
                        a = group(i)
                        dve.tensor_tensor(a, a, mu.unsqueeze(1).broadcast_to([P, TB, D]), ALU.subtract).then_inc(s_c, 1)
                    dve.wait_ge(s_m, 2 * NG)
                    link(dve.tensor_scalar(mu, psum[1][:, 0:D], 1.0 / N, None, ALU.mult))
                    dve.wait_ge(s_sq, NG + 1)
                    link(dve.reciprocal(mu, mu))
                    link(dve.tensor_tensor(bn_g, bn_g, mu, ALU.mult))
                    if add_to_x:
                        for g_ in range(NG):
                            a = acc[:, g_ * TB:(g_ + 1) * TB, 0:D]
                            xs = xres[:, g_ * TB:(g_ + 1) * TB, :]
                            link(dve.tensor_tensor(a, a, bn_g.unsqueeze(1).broadcast_to([P, TB, D]), ALU.mult))
                            link(dve.tensor_tensor(a, a, bn_b.unsqueeze(1).broadcast_to([P, TB, D]), ALU.add))
                            link(dve.tensor_tensor(xs, xs, a, ALU.add))

                @block.scalar
                def _(act):
                    with act.Fori(0, NG) as i:
                        act.wait_ge(s_z, (i + 1) * TB)
                        act.activation(group(i), group(i), ACT.Relu).then_inc(s_r, 1)
                    for g_ in range(NG):
                        act.wait_ge(s_c, g_ + 1)
                        if g_:
                            act.wait_ge(s_m, NG + g_)
                        act.activation(y_ring, acc[:, g_ * TB:(g_ + 1) * TB, 0:D], ACT.Square).then_inc(s_sq, 1)
                    act.wait_ge(s_v, 2)
                    act.activation(mu, mu, ACT.Sqrt, bias=eps[:, 0:1]).then_inc(s_sq, 1)

                @block.tensor
                def _(pe):
                    column_sums(pe, 0, lambda t, u: acc[:, t, 0:D], s_r, lambda g_: g_ + 1)
                    column_sums(pe, 1, lambda t, u: y_ring[:, u, :], s_sq, lambda g_: g_ + 1)

        row_stats("ln1")
        project("gate0", NE, gate_w, {"act": layernorm_rows}, {"dve": take_logits}, load_gate(f0_gw, f0_gb), 32)
        route("route0", 1, CAP)
        dispatch("send0", 1, TILES0)
        experts("ffn0", TILES0, f0_w1, f0_b1, f0_w2, f0_b2, ACT.Relu, None)
        combine("back0", 1, TILES0, False)

        reuse_semaphores()
        row_stats("ln2")
        project("gcn0", D, wproj, {"act": layernorm_rows}, {"act": gcn_out}, load_w(g1_w0), 16, store=gcn_store)
        walk("gcn0_walk", False)
        batch_stats("bn0", g1_b0, g1_g0, g1_bt0, False)
        project("gcn1", D, wproj, {"dve": batchnorm_rows}, {"act": gcn_out}, load_w(g1_w1), 16, store=gcn_store)
        walk("gcn1_walk", False)
        batch_stats("bn1", g1_b1, g1_g1, g1_bt1, True)

        reuse_semaphores()
        row_stats("ln3")
        project("gate1", NE, gate_w, {"act": layernorm_rows}, {"dve": take_logits}, load_gate(f1_wr, f1_br), 32)
        route("route1", 2, 1 << 20)
        dispatch("send1", 2, TILES1)
        experts("ffn1", TILES1, f1_w1, f1_b1, f1_w2, f1_b2, ACT.Gelu, (f1_lg, f1_lb))
        combine("back1", 2, TILES1, True)


_INS = ["x", "src", "dst", "L0_gnn_W", "L0_gnn_attn_l", "L0_gnn_attn_r", "L0_gnn_bias", "L0_ffn_gate_w",
        "L0_ffn_gate_b", "L0_ffn_w1", "L0_ffn_b1", "L0_ffn_w2", "L0_ffn_b2", "L1_gnn_W0", "L1_gnn_b0",
        "L1_gnn_g0", "L1_gnn_bt0", "L1_gnn_W1", "L1_gnn_b1", "L1_gnn_g1", "L1_gnn_bt1", "L1_ffn_Wr",
        "L1_ffn_br", "L1_ffn_ln_g", "L1_ffn_ln_b", "L1_ffn_W1", "L1_ffn_b1", "L1_ffn_W2", "L1_ffn_b2"]


def kernel(**inputs):
    import concourse.bacc as bacc
    from concourse.bass_utils import run_bass_kernel_spmd

    nc = bacc.Bacc("TRN2", target_bir_lowering=False, num_devices=1)
    arrays, args = {}, []
    for name in _INS:
        a = np.ascontiguousarray(inputs[name])
        arrays[f"in_{name}"] = a
        args.append(nc.dram_tensor(f"in_{name}", a.shape, mybir.dt.from_np(a.dtype), kind="ExternalInput").ap())
    args.append(nc.dram_tensor("out_x", (N, D), F32, kind="ExternalOutput").ap())
    build(nc, *args)
    return run_bass_kernel_spmd(nc, [arrays], core_ids=[0]).results[0]["out_x"]
```

```python
import math
from contextlib import ExitStack

import numpy as np
import concourse.bass as bass
from concourse import mybir

F32 = mybir.dt.float32
I32 = mybir.dt.int32
BF16 = mybir.dt.bfloat16
ALU = mybir.AluOpType
ACT = mybir.ActivationFunctionType
AX_X = mybir.AxisListType.X
RMAX = bass.bass_isa.ReduceOp.max

P = 128
D = 256
KC = D // P
N = 6250
NT = math.ceil(N / P)
LAST = N - (NT - 1) * P
TB = 7
NG = NT // TB
AHEAD = 4
TURN = (0, 1, 2, 0, 1, 2, 1)
HEADS = 4
HD = D // HEADS
E = 200000
EB = 256
NB = math.ceil(E / EB)
NBP = NB + 2
UN = 8
RB = 4
PAIRS = math.ceil((NB + NT - 1) / UN) * UN
STEPS = PAIRS // UN
PCH = math.ceil(PAIRS / P)
PCOL = PCH * P
AW = 264
GW = D + HEADS
MW = GW + 1
NE = 8
FF = 1024
FC = FF // P
CAP = math.ceil(1.25 * N / NE)
TILES0 = (N + NE * (P - 1)) // P
TILES1 = (2 * N + NE * (P - 1)) // P
TILES0 += TILES0 % 2
TILES1 += TILES1 % 2
LN_EPS = 1e-5
FMAX = 3.4028234e38
SPAN = 60.0
ARENA = 30720
assert NG * TB == NT


def wait(eng, sem, value):
    if isinstance(value, int) and value <= 0:
        return
    eng.wait_ge(sem, value)


def rolled(eng, count, body):
    body(0)
    with eng.Fori(1, count) as i:
        body(i)


class Chain:

    def __init__(self, eng, sem):
        self.eng, self.sem, self.n = eng, sem, 0

    def __call__(self, ins):
        self.n += 1
        ins.then_inc(self.sem, 1)
        self.eng.wait_ge(self.sem, self.n)


def build(nc, x, src, dst, g0_w, g0_al, g0_ar, g0_bias, f0_gw, f0_gb, f0_w1, f0_b1, f0_w2, f0_b2,
          g1_w0, g1_b0, g1_g0, g1_bt0, g1_w1, g1_b1, g1_g1, g1_bt1, f1_wr, f1_br, f1_lg, f1_lb,
          f1_w1, f1_b1, f1_w2, f1_b2, out):
    src_pad = nc.dram_tensor("src_pad", [NBP * EB], I32).ap()
    dst_pad = nc.dram_tensor("dst_pad", [NBP * EB], I32).ap()
    src_cols = nc.dram_tensor("src_cols", [P, PCOL * 2], I32).ap()
    dst_cols = nc.dram_tensor("dst_cols", [P, PCOL * 2], F32).ap()
    table0 = nc.dram_tensor("table0", [NT * P, AW], F32).ap()
    table1 = nc.dram_tensor("table1", [NT * P, D], F32).ap()
    expert_in = nc.dram_tensor("expert_in", [TILES1 * P, D], F32).ap()
    expert_out = nc.dram_tensor("expert_out", [TILES1 * P, D], F32).ap()

    def rows(a, lo, hi):
        return a[lo * P:hi * P, :].rearrange("(t p) d -> p t d", p=P)

    with ExitStack() as ctx:
        ctx.enter_context(nc.allow_non_contiguous_dma(reason="a few short index and bias loads"))

        def sb(name, shape, dt=F32):
            return ctx.enter_context(nc.sbuf_tensor(name, shape, dt))

        taken = []

        def sem(name):
            taken.append(nc.alloc_semaphore(name=name))
            return taken[-1]

        def reuse_semaphores():
            nc.clear_and_free_semaphores(taken)
            taken.clear()
            nc.all_engine_barrier()

        psum = [ctx.enter_context(nc.psum_tensor(f"bank{i}", [P, 512], F32)) for i in range(8)]

        xres = sb("xres", [P, NT, D])
        xflat = xres[:, :, :].rearrange("p t d -> p (t d)")
        arena = sb("arena", [P, ARENA])
        used = [0]

        def room(width):
            used[0] += width
            return arena[:, used[0] - width:used[0]]

        acc_flat = room(NT * AW)
        acc = acc_flat.rearrange("p (t d) -> p t d", t=NT)
        src_sb = room(PCOL * 2).bitcast(I32)
        dst_sb = room(PCOL * 2)
        onehot = room(UN * EB).rearrange("p (u j n) -> p u j n", u=UN, j=2)
        got = room(UN * 2 * AW).rearrange("p (u j n) -> p u j n", u=UN, j=2)
        msg = room(RB * 2 * AW).rearrange("p (u j n) -> p u j n", u=RB, j=2)
        wproj = room(KC * AW).rearrange("p (c n) -> p c n", c=KC)
        wraw = room(KC * D).rearrange("p (c n) -> p c n", c=KC)
        attn = room(2 * D).rearrange("p (a n) -> p a n", a=2)
        bias_bc = room(D)
        er_u = room(NT * 8).rearrange("p (t n) -> p t n", t=NT)
        el_all = room(NT * HEADS).rearrange("p (t n) -> p t n", t=NT)
        peak_at = used[0]
        peak = room(NT * HEADS).rearrange("p (t n) -> p t n", t=NT)
        parts_at = 2 * used[0]
        arena16 = arena[:, :].bitcast(BF16)
        er_parts = room(NT * 12).bitcast(BF16).rearrange("p (t k n) -> p t k n", t=NT, k=3)
        y_at = ARENA - NT * D
        y_all = arena[:, y_at:]
        pick_a = arena[:, 0:NT * D].rearrange("p (t d) -> p t d", t=NT)
        pick_b = arena[:, NT * D:2 * NT * D].rearrange("p (t d) -> p t d", t=NT)
        clean_at = 2 * NT * D
        W2W = NE * FC * D
        assert W2W <= y_at
        w2_sb = arena[:, 0:W2W].rearrange("p (e c d) -> p e c d", e=NE, c=FC)
        w1_ring = arena[:, W2W:W2W + 2 * KC * FF].rearrange("p (s c f) -> p s c f", s=2, c=KC)
        b2_bc = arena[:, W2W + 2 * KC * FF:W2W + 2 * KC * FF + NE * D]

        ident = sb("ident", [P, P])
        ones = sb("ones", [P, P])
        tri = sb("tri", [P, P])
        iota_n = sb("iota_n", [P, P])
        rings = sb("rings", [P, TB * (D + AW)])
        y_ring = rings[:, 0:TB * D].rearrange("p (t d) -> p t d", t=TB)
        yt_ring = sb("yt_ring", [P, 3, D])
        stage_flat = rings[:, TB * D:]
        stage = stage_flat.rearrange("p (t d) -> p t d", t=TB)
        onehot_t = stage_flat[:, 0:RB * P].bitcast(BF16).rearrange("p (u j n) -> p u j n", u=RB, j=2)
        hmid = rings[:, 0:2 * FF].rearrange("p (s c n) -> p s c n", s=2, c=FC)
        x_in = rings[:, 2 * FF:2 * FF + 2 * D].rearrange("p (s d) -> p s d", s=2)
        y_out = rings[:, 2 * FF + 2 * D:2 * FF + 4 * D].rearrange("p (s d) -> p s d", s=2)
        b1_sb = sb("b1_sb", [P, NE, FC])
        lg_sb = sb("lg_sb", [P, KC, NE])
        lb_sb = sb("lb_sb", [P, KC, NE])
        bn_g = room(D)
        bn_b = room(D)
        stats = sb("stats", [P, NT, 6])
        lnt = sb("lnt", [P, 6, NT])
        mean, rstd, nmr = lnt[:, 0, :], lnt[:, 1, :], lnt[:, 2, :]
        dis = sb("dis", [P, NT])
        small = sb("small", [P, 64])
        eps = sb("eps", [P, 1])
        tile_one = sb("tile_one", [P, 1])
        valid = sb("valid", [P, NT])
        gate_w = sb("gate_w", [P, KC, NE])
        gate_b = sb("gate_b", [P, NE])
        iota_e = sb("iota_e", [P, NE])
        logit = sb("logit", [P, NT, NE])
        slot = sb("slot", [P, 4, NT], I32)
        wgt = sb("wgt", [P, 2, NT])
        idx_ring = sb("idx_ring", [P, 2 * UN], I32)
        tpack = sb("tpack", [1, PAIRS // 4], I32)
        tile_e = sb("tile_e", [1, P], I32)
        wide = sb("wide", [1, 1], I32)

        def cols(a, c):
            return a[:, c * P:(c + 1) * P]

        def own(a, v):
            return a[:, bass.ds(v, 1)]

        k_c, k_x, k_pad = sem("k_c"), sem("k_x"), sem("k_pad")
        with nc.Block() as block:
            @block.gpsimd
            def _(pool):
                link = Chain(pool, k_c)
                link(pool.memset(ident[:, :], 0.0))
                link(pool.affine_select(out=ident[:, :], in_=ident[:, :], compare_op=ALU.not_equal, fill=1.0,
                                        base=0, pattern=[[-1, P]], channel_multiplier=1))
                link(pool.memset(ones[:, :], 1.0))
                link(pool.affine_select(out=tri[:, :], in_=ones[:, :], compare_op=ALU.is_ge, fill=0.0,
                                        base=0, pattern=[[1, P]], channel_multiplier=-1))
                link(pool.iota(iota_n[:, :], pattern=[[1, P]], base=0, channel_multiplier=0,
                               allow_small_or_imprecise_dtypes=True))
                link(pool.iota(iota_e[:, :], pattern=[[1, NE]], base=0, channel_multiplier=0,
                               allow_small_or_imprecise_dtypes=True))
                link(pool.memset(eps[:, :], LN_EPS))
                link(pool.affine_select(out=tile_one[:, :], in_=ones[:, 0:1], compare_op=ALU.is_ge, fill=0.0,
                                        base=-1, pattern=[[0, 1]], channel_multiplier=1))
                link(pool.memset(valid[:, :], 1.0))
                link(pool.affine_select(out=valid[:, NT - 1:NT], in_=ones[:, 0:1], compare_op=ALU.is_ge, fill=0.0,
                                        base=LAST - 1, pattern=[[0, 1]], channel_multiplier=-1))
                link(pool.memset(xres[:, NT - 1, :], 0.0))
                link(pool.memset(idx_ring[:, 0:4], 0))
                link(pool.memset(idx_ring[:, 4:8], 1 << 20))

            @block.sync
            def _(sp):
                sp.dma_start(src_pad[0:E].rearrange("(a b) -> a b", a=16),
                             src.rearrange("(a b) -> a b", a=16)).then_inc(k_pad, 16)
                sp.dma_start(dst_pad[0:E].rearrange("(a b) -> a b", a=16),
                             dst.rearrange("(a b) -> a b", a=16)).then_inc(k_pad, 16)
                for t in range(0, NT - 1, 8):
                    sp.dma_start(xres[:, t:t + 8, :], rows(x, t, t + 8)).then_inc(k_x, 16)
                sp.wait_ge(k_c, 13)
                pad = NBP * EB - E
                rowsp = pad // 4
                done = 0
                while done < rowsp:
                    n = min(P, rowsp - done)
                    lo = E + 4 * done
                    for to, c in ((src_pad, 0), (dst_pad, 4)):
                        sp.dma_start(to[lo:lo + 4 * n].rearrange("(a b) -> a b", b=4),
                                     idx_ring[0:n, c:c + 4]).then_inc(k_pad, 16)
                    done += n
                sp.dma_start(xres[0:LAST, NT - 1, :], x[(NT - 1) * P:N, :]).then_inc(k_x, 16)
                sp.wait_ge(k_pad, 16 * (2 + 2 * math.ceil(rowsp / P)))
                sp.wait_ge(k_x, 16 * ((NT - 1) // 8 + 1))

        q_in, q_c, q_pe, q_g, q_t, q_o, q_v, q_z, q_zero = (sem(n) for n in
            ("q_in", "q_c", "q_pe", "q_g", "q_t", "q_o", "q_v", "q_z", "q_zero"))
        HB = NBP // 2
        last_i = acc_flat[0:1, 0:NBP].bitcast(I32)
        last_f = acc_flat[0:1, NBP:2 * NBP]
        below = acc_flat[0:P, 2 * NBP:3 * NBP]
        base = 3 * NBP
        tlow = acc_flat[:, base:base + 1]
        tnum = acc_flat[:, base + 1:base + 2]
        pstart = acc_flat[:, base + 2:base + 3]
        piota = acc_flat[:, base + 8:base + 8 + PCOL]
        ind = acc_flat[:, base + 8 + PCOL:base + 8 + 2 * PCOL]
        b2 = base + 8 + 2 * PCOL
        pcol = acc_flat[:, b2:b2 + PCH]
        tcol = acc_flat[:, b2 + 8:b2 + 8 + PCH]
        bcol = acc_flat[:, b2 + 16:b2 + 16 + PCH]
        bidx = acc_flat[:, b2 + 24:b2 + 24 + PCH].bitcast(I32)
        lowcol = acc_flat[:, b2 + 32:b2 + 32 + PCH]
        b3 = b2 + 64
        raw = acc_flat[:, b3:b3 + 2 * PCH * EB].bitcast(I32).rearrange("p (a k e) -> p a k e", a=2, k=PCH)
        b4 = b3 + 2 * PCH * EB
        cooked = acc_flat[:, b4:b4 + 2 * PCH * EB].rearrange("p (a k e) -> p a k e", a=2, k=PCH)
        trow = acc_flat[0:1, b4 + 2 * PCH * EB:b4 + 2 * PCH * EB + PCOL]
        assert b4 + 2 * PCH * EB + PCOL <= NT * AW
        with nc.Block() as block:
            @block.sync
            def _(sp):
                sp.dma_start(last_i.rearrange("a (b c) -> a b c", c=1),
                             dst_pad.rearrange("(a b c) -> a b c", a=1, c=EB)[:, :, EB - 1:EB]).then_inc(q_in, 16)
                sp.wait_ge(q_z, 1)
                for t in range(0, TILES1, TB):
                    n = min(TB, TILES1 - t)
                    sp.dma_start(rows(expert_in, t, t + n), y_ring[:, 0:n, :]).then_inc(q_zero, 16)
                sp.wait_ge(q_zero, 16 * math.ceil(TILES1 / TB))
                sp.wait_ge(q_t, 4 * PCH)
                sp.dma_start(src_cols, src_sb).then_inc(q_o, 16)
                sp.dma_start(dst_cols, dst_sb).then_inc(q_o, 16)
                sp.wait_ge(q_o, 32)

            @block.gpsimd
            def _(pool):
                link = Chain(pool, q_c)
                link(pool.iota(tlow, pattern=[[0, 1]], base=0, channel_multiplier=P,
                               allow_small_or_imprecise_dtypes=True))
                link(pool.iota(tnum, pattern=[[0, 1]], base=0, channel_multiplier=1,
                               allow_small_or_imprecise_dtypes=True))
                link(pool.iota(piota, pattern=[[1, PCOL]], base=0, channel_multiplier=0,
                               allow_small_or_imprecise_dtypes=True))
                link(pool.iota(pcol, pattern=[[P, PCH]], base=0, channel_multiplier=1,
                               allow_small_or_imprecise_dtypes=True))
                pool.wait_ge(q_v, 9)
                for k in range(PCH):
                    for a, table in enumerate((src_pad, dst_pad)):
                        pool.indirect_dma_start(out=raw[:, a, k, :], out_offset=None,
                                                in_=table.rearrange("(b e) -> b e", e=EB),
                                                in_offset=bass.IndirectOffsetOnAxis(ap=bidx[:, k:k + 1], axis=0)
                                                ).then_inc(q_g, 16)

            @block.vector
            def _(dve):
                dve.memset(y_ring, 0.0).then_inc(q_z, 1)
                link = Chain(dve, q_v)
                dve.wait_ge(q_in, 16)
                link(dve.tensor_copy(last_f, last_i))
                dve.wait_ge(q_pe, 1)
                dve.wait_ge(q_c, 4)
                for h in range(2):
                    dve.tensor_scalar(below[:, h * HB:(h + 1) * HB], psum[h][:, 0:HB], tlow, None,
                                      ALU.is_lt).then_inc(q_v, 1)
                dve.wait_ge(q_v, 3)
                link.n = 3
                link(dve.reduce_sum(pstart, below, AX_X))
                link(dve.tensor_tensor(pstart, pstart, tnum, ALU.add))
                link(dve.tensor_scalar(ind, piota, pstart, None, ALU.is_ge))
                dve.wait_ge(q_pe, 2)
                link(dve.tensor_copy(tcol, psum[2][:, 0:PCH]))
                link(dve.tensor_tensor(bcol, pcol, tcol, ALU.subtract))
                link(dve.tensor_scalar(bidx, bcol, float(NBP - 1), None, ALU.min))
                link(dve.tensor_scalar(lowcol, tcol, float(P), None, ALU.mult))
                for h in range(2):
                    link(dve.tensor_copy(trow[:, h * (PCOL // 2):(h + 1) * (PCOL // 2)],
                                         psum[3 + h][0:1, 0:PCOL // 2]))
                four = trow[:, 0:PAIRS].rearrange("p (s u) -> p u s", u=4)
                link(dve.scalar_tensor_tensor(out=below[0:1, 0:PAIRS // 4], in0=four[:, 3, :], scalar=64.0,
                                              in1=four[:, 2, :], op0=ALU.mult, op1=ALU.add))
                link(dve.scalar_tensor_tensor(out=below[0:1, 0:PAIRS // 4], in0=below[0:1, 0:PAIRS // 4], scalar=64.0,
                                              in1=four[:, 1, :], op0=ALU.mult, op1=ALU.add))
                link(dve.scalar_tensor_tensor(out=tpack[0:1, :], in0=below[0:1, 0:PAIRS // 4], scalar=64.0,
                                              in1=four[:, 0, :], op0=ALU.mult, op1=ALU.add))
                dve.wait_ge(q_g, 16 * 2 * PCH)
                for k in range(PCH):
                    dve.tensor_copy(cooked[:, 0, k, :], raw[:, 0, k, :]).then_inc(q_v, 1)
                    dve.tensor_scalar(cooked[:, 1, k, :], raw[:, 1, k, :], lowcol[:, k:k + 1], None,
                                      ALU.subtract).then_inc(q_v, 1)
                for k in range(PCH):
                    for a, to in enumerate((src_sb, dst_sb)):
                        for j in range(2):
                            n = (2 * k + a) * 2 + j
                            dve.wait_ge(q_pe, 3 + n)
                            dve.tensor_copy(to.rearrange("p (c j) -> p j c", j=2)[:, j, k * P:(k + 1) * P],
                                            psum[n % 8][:, 0:P]).then_inc(q_t, 1)

            @block.tensor
            def _(pe):
                pe.wait_ge(q_v, 1)
                for h in range(2):
                    last = pe.matmul(psum[h][:, 0:HB], ones[0:1, :], last_f[:, h * HB:(h + 1) * HB],
                                     start=True, stop=True)
                last.then_inc(q_pe, 1)
                pe.wait_ge(q_v, 6)
                for k in range(PCH):
                    pe.matmul(psum[2][:, k:k + 1], ind[0:NT, k * P:(k + 1) * P], tile_one[0:NT, 0:1],
                              start=True, stop=True)
                for h in range(2):
                    last = pe.matmul(psum[3 + h][0:1, 0:PCOL // 2], tile_one[0:NT, 0:1],
                                     ind[0:NT, h * (PCOL // 2):(h + 1) * (PCOL // 2)], start=True, stop=True)
                last.then_inc(q_pe, 1)
                pe.wait_ge(q_v, 15 + 2 * PCH)
                for k in range(PCH):
                    for a in range(2):
                        for j in range(2):
                            n = (2 * k + a) * 2 + j
                            if n >= 8:
                                pe.wait_ge(q_t, n - 7)
                            pe.transpose(psum[n % 8][:, 0:P], cooked[:, a, k, j * P:(j + 1) * P],
                                         ident[:, :]).then_inc(q_pe, 1)

        def row_stats(tag):
            s_st, s_v, s_sq = sem(tag + "_st"), sem(tag + "_v"), sem(tag + "_sq")
            t_a, t_b, var = lnt[:, 3, :], lnt[:, 4, :], lnt[:, 5, :]
            with nc.Block() as block:
                @block.vector
                def _(dve):
                    with dve.Fori(0, NG) as i:
                        for u in range(TB):
                            t = i * TB + u
                            dve.bn_stats(stats[:, bass.ds(t, 1), :], xflat[:, bass.ds(t * D, D)]).then_inc(s_st, 1)
                    dve.wait_ge(s_st, NT)
                    link = Chain(dve, s_v)
                    me, ve, mo, vo = (stats[:, :, c] for c in (1, 2, 4, 5))
                    link(dve.tensor_tensor(t_a, me, mo, ALU.add))
                    link(dve.tensor_scalar(mean, t_a, 0.5, None, ALU.mult))
                    link(dve.tensor_tensor(t_a, me, mo, ALU.subtract))
                    link(dve.scalar_tensor_tensor(out=t_b, in0=t_a, scalar=0.25, in1=t_a, op0=ALU.mult, op1=ALU.mult))
                    link(dve.tensor_tensor(t_a, ve, vo, ALU.add))
                    link(dve.scalar_tensor_tensor(out=var, in0=t_a, scalar=1.0 / D, in1=t_b,
                                                  op0=ALU.mult, op1=ALU.add))
                    dve.wait_ge(s_sq, 1)
                    link(dve.reciprocal(rstd, t_a))
                    link(dve.scalar_tensor_tensor(out=nmr, in0=mean, scalar=-1.0, in1=rstd,
                                                  op0=ALU.mult, op1=ALU.mult))

                @block.scalar
                def _(act):
                    act.wait_ge(s_v, 6)
                    act.activation(t_a, var, ACT.Sqrt, bias=eps[:, 0:1]).then_inc(s_sq, 1)

        def project(tag, width, w_sb, rows_of, evac, load, n_load, before=None, n_before=0, store=None):
            s = {n: sem(tag + "_" + n) for n in ("w", "y", "t", "yt", "f", "e", "b", "q", "h")}
            s["out"] = [sem(f"{tag}_out{u}") for u in range(TB)]
            with nc.Block() as block:
                @block.sync
                def _(sp):
                    load(sp, s["w"])
                    if store:
                        rolled(sp, NG, lambda i: [store(sp, s, i, u) for u in range(TB)])
                        for u in range(TB):
                            sp.wait_ge(s["out"][u], 16 * NG)

                def groups(eng, body):
                    body(0)
                    with eng.Fori(1, NG - 1) as i:
                        body(i)
                    body(NG - 1)

                def rows_ahead(eng, make, i, u):
                    v = u + AHEAD
                    if v < TB:
                        make(eng, s, i * TB + v, v)
                    elif not (isinstance(i, int) and i == NG - 1):
                        make(eng, s, (i + 1) * TB + v - TB, v - TB)

                @block.scalar
                def _(act):
                    rows = rows_of.get("act")

                    def fill(eng, s, k, u):
                        wait(eng, s["t"], k - TB + 1)
                        rows(eng, s, k, u)

                    def body(i):
                        for u in range(TB):
                            if rows:
                                rows_ahead(act, fill, i, u)
                            if "act" in evac:
                                evac["act"](act, s, i, u)
                    if rows:
                        for u in range(AHEAD):
                            fill(act, s, u, u)
                    groups(act, body)

                @block.vector
                def _(dve):
                    rows = rows_of.get("dve")
                    if before:
                        before(dve, s)

                    def transposed(i, u):
                        k = i * TB + u
                        dve.wait_ge(s["t"], k + 1)
                        wait(dve, s["f"], k - 1)
                        dve.tensor_copy(yt_ring[:, TURN[u], :], psum[TURN[u]][:, 0:D]).then_inc(s["yt"], 1)

                    def body(i):
                        for u in range(TB):
                            if rows:
                                rows_ahead(dve, rows, i, u)
                            transposed(i, u)
                            if "dve" in evac:
                                if u:
                                    evac["dve"](dve, s, i, u - 1)
                                elif not (isinstance(i, int) and i == 0):
                                    evac["dve"](dve, s, i - 1, TB - 1)
                    if rows:
                        for u in range(AHEAD):
                            rows(dve, s, u, u)
                    groups(dve, body)
                    if "dve" in evac:
                        evac["dve"](dve, s, NG - 1, TB - 1)

                @block.tensor
                def _(pe):
                    pe.wait_ge(s["w"], n_load)
                    wait(pe, s["b"], n_before)

                    def turn(i, u):
                        k = i * TB + u
                        pe.wait_ge(s["y"], k + 1)
                        wait(pe, s["yt"], k - 1)
                        for c in range(KC):
                            last = pe.transpose(psum[TURN[u]][:, c * P:(c + 1) * P],
                                                cols(y_ring[:, u, :], c), ident[:, :])
                        last.then_inc(s["t"], 1)

                    def product(i, u):
                        k = i * TB + u
                        pe.wait_ge(s["yt"], k + 1)
                        wait(pe, s["e"], k - 1)
                        for c in range(KC):
                            last = pe.matmul(psum[3 + TURN[u]][:, 0:width], yt_ring[:, TURN[u], c * P:(c + 1) * P],
                                             w_sb[:, c, 0:width], start=(c == 0), stop=(c == KC - 1))
                        last.then_inc(s["f"], 1)

                    def body(i):
                        for u in range(TB):
                            turn(i, u)
                            if u:
                                product(i, u - 1)
                            elif not (isinstance(i, int) and i == 0):
                                product(i - 1, TB - 1)
                    groups(pe, body)
                    product(NG - 1, TB - 1)

        def layernorm_rows(act, s, t, u):
            act.activation(y_ring[:, u, :], xflat[:, bass.ds(t * D, D)], ACT.Identity,
                           bias=own(nmr, t), scale=own(rstd, t)).then_inc(s["y"], 1)

        def walk(tag, attention):
            table, gw = (table0, AW) if attention else (table1, D)
            mw = MW if attention else D
            s_in, s_oh, s_t, s_ht, s_b, s_z, s_w, s_m, s_a, s_acc, s_idx, s_c, s_one = (
                sem(tag + "_" + n) for n in ("in", "oh", "t", "ht", "b", "z", "w", "m", "a", "acc", "idx", "c", "one"))
            s_g = [sem(f"{tag}_g{u}") for u in range(UN)]
            s_go = sem(tag + "_go")
            zt = small[:, :].rearrange("p (u j h) -> p u j h", u=RB, j=2)
            banks_t = [psum[u % 2][:, 0:EB] for u in range(UN)]
            banks_e = [psum[2 + u % 2][:, 0:16].rearrange("p (j h) -> p j h", j=2) for u in range(UN)]
            banks_a = [psum[4 + u % RB] for u in range(UN)]

            def final(i):
                return isinstance(i, int) and i == STEPS - 1

            def steps(eng, body):
                body(0)
                with eng.Fori(1, STEPS - 1) as i:
                    body(i)
                body(STEPS - 1)

            def gather(pool, u):
                for j in range(2):
                    pool.indirect_dma_start(out=got[:, u, j, 0:gw], out_offset=None, in_=table,
                                            in_offset=bass.IndirectOffsetOnAxis(
                                                ap=idx_ring[:, 2 * u + j:2 * u + j + 1], axis=0)
                                            ).then_inc(s_g[u], 16)

            def tiles_of(eng, i):
                words = [eng.value_load(tpack[0:1, bass.ds(i * (UN // 4) + w, 1)], min_val=0, max_val=(1 << 24) - 1)
                         for w in range(UN // 4)]
                return lambda u: eng.snap((words[u // 4] // (1 << (6 * (u % 4)))) % 64)

            with nc.Block() as block:
                @block.sync
                def _(sp):
                    sp.dma_start(src_sb, src_cols).then_inc(s_in, 16)
                    sp.dma_start(dst_sb, dst_cols).then_inc(s_in, 16)

                @block.gpsimd
                def _(pool):
                    def step(i, u):
                        pool.wait_ge(s_idx, UN * i + u + 1)
                        wait(pool, s_m if attention else s_a, UN * (i - 1) + u + 1)
                        pool.sem_inc(s_go, 1)
                        gather(pool, u)
                    rolled(pool, STEPS, lambda i: [step(i, u) for u in range(UN)])

                @block.scalar
                def _(act):
                    def stage_idx(i, u):
                        c = 2 * (UN * (i + 1) + u)
                        if not (isinstance(i, int) and i < 0):
                            act.wait_ge(s_g[u], 32 * (i + 1))
                        act.copy(idx_ring[:, 2 * u:2 * u + 2], src_sb[:, bass.ds(c, 2)]).then_inc(s_idx, 1)

                    def copy_onehot(i, u):
                        act.wait_ge(s_t, UN * i + u + 1)
                        act.copy(onehot_t[:, u % RB, :, :].rearrange("p j n -> p (j n)"), banks_t[u]).then_inc(s_ht, 1)

                    def weights(i, u):
                        act.wait_ge(s_z, UN * i + u + 1)
                        act.activation(msg[:, u % RB, :, D:GW], zt[:, u % RB, :, 0:4], ACT.Exp).then_inc(s_w, 1)

                    act.wait_ge(s_in, 32)
                    for u in range(UN):
                        stage_idx(-1, u)
                    if attention:
                        copy_onehot(0, 0)

                    def body(i):
                        for u in range(UN):
                            if attention:
                                if u + 1 < UN:
                                    copy_onehot(i, u + 1)
                                elif not final(i):
                                    copy_onehot(i + 1, 0)
                                weights(i, u)
                            if not final(i):
                                stage_idx(i, u)
                    steps(act, body)

                @block.vector
                def _(dve):
                    def make_onehot(i, u):
                        c = 2 * (UN * i + u)
                        dve.tensor_tensor(onehot[:, u, :, :], iota_n[:, :].unsqueeze(1).broadcast_to([P, 2, P]),
                                          dst_sb[:, bass.ds(c, 2)].unsqueeze(2).broadcast_to([P, 2, P]),
                                          ALU.is_equal).then_inc(s_oh, 1)

                    def score_sum(i, u):
                        dve.wait_ge(s_b, UN * i + u + 1)
                        dve.wait_ge(s_g[u], 32 * (i + 1))
                        wait(dve, s_w, UN * i + u - RB + 1)
                        dve.tensor_tensor(zt[:, u % RB, :, :], got[:, u, :, D:AW], banks_e[u], ALU.add).then_inc(s_c, 1)

                    def score_max(i, u):
                        dve.wait_ge(s_c, 2 * (UN * i + u) + 1)
                        dve.tensor_tensor(zt[:, u % RB, :, 0:4], zt[:, u % RB, :, 0:4], zt[:, u % RB, :, 4:8],
                                          ALU.max).then_inc(s_c, 1)

                    def score_clamp(i, u):
                        z = zt[:, u % RB, :, 0:4]
                        dve.wait_ge(s_c, 2 * (UN * i + u) + 2)
                        dve.tensor_scalar(z, z, 0.0, None, ALU.min).then_inc(s_z, 1)

                    def messages(i, u, j):
                        if j == 0:
                            dve.wait_ge(s_w, UN * i + u + 1)
                        done = dve.tensor_tensor(
                            msg[:, u % RB, j, 0:D].rearrange("p (h d) -> p h d", h=HEADS),
                            got[:, u, j, 0:D].rearrange("p (h d) -> p h d", h=HEADS),
                            msg[:, u % RB, j, D:GW].unsqueeze(2).broadcast_to([P, HEADS, HD]), ALU.mult)
                        if j == 1:
                            done.then_inc(s_m, 1)

                    def collect(i, u, t):
                        n = UN * i + u
                        dve.wait_ge(s_a, n + 1)
                        wait(dve, s_acc, n)
                        cell = arena[:, bass.ds(t * AW, mw)]
                        dve.tensor_tensor(cell, cell, banks_a[u][:, 0:mw], ALU.add).then_inc(s_acc, 1)

                    if attention:
                        dve.memset(msg[:, :, :, GW:AW], 1.0).then_inc(s_one, 1)
                    dve.wait_ge(s_in, 32)
                    for u in range(UN):
                        make_onehot(0, u)
                    if attention:
                        for u in range(2):
                            score_sum(0, u)
                            score_max(0, u)
                            score_clamp(0, u)
                        messages(0, 0, 0)
                        messages(0, 0, 1)

                    def body(i):
                        tile = tiles_of(dve, i)
                        for u in range(UN):
                            two = attention and (u + 2 < UN or not final(i)) and (i + (u + 2) // UN, (u + 2) % UN)
                            one = attention and (u + 1 < UN or not final(i)) and (i + (u + 1) // UN, (u + 1) % UN)
                            if two:
                                score_sum(*two)
                            if one:
                                messages(*one, 0)
                            if two:
                                score_max(*two)
                            if one:
                                messages(*one, 1)
                            if two:
                                score_clamp(*two)
                            collect(i, u, tile(u))
                            if not final(i):
                                make_onehot(i + 1, u)
                    steps(dve, body)

                @block.tensor
                def _(pe):
                    def turn(i, u):
                        pe.wait_ge(s_oh, UN * i + u + 1)
                        wait(pe, s_ht, UN * i + u - 1)
                        for j in range(2):
                            last = pe.transpose(banks_t[u][:, j * P:(j + 1) * P], onehot[:, u, j, :], ident[:, :])
                        last.then_inc(s_t, 1)

                    def spread(i, u, t):
                        pe.wait_ge(s_ht, UN * i + u + 1)
                        wait(pe, s_z, UN * i + u - 1)
                        for j in range(2):
                            for k in range(3):
                                last = pe.matmul(banks_e[u][:, j, :], onehot_t[:, u % RB, j, :],
                                                 arena16[:, bass.ds(t * 24 + (parts_at + 8 * k), 8)],
                                                 start=(k == 0), stop=(k == 2))
                        last.then_inc(s_b, 1)

                    def add_up(i, u):
                        n = UN * i + u
                        if attention:
                            pe.wait_ge(s_m, n + 1)
                        else:
                            pe.wait_ge(s_oh, n + 1)
                            pe.wait_ge(s_g[u], 32 * (i + 1))
                        wait(pe, s_acc, n - RB + 1)
                        for j in range(2):
                            last = pe.matmul(banks_a[u][:, 0:mw], onehot[:, u, j, :],
                                             msg[:, u % RB, j, 0:mw] if attention else got[:, u, j, 0:mw],
                                             start=(j == 0), stop=(j == 1))
                        last.then_inc(s_a, 1)

                    if attention:
                        pe.wait_ge(s_one, 1)
                        turn(0, 0)

                        def body(i):
                            tile = tiles_of(pe, i)
                            for u in range(UN):
                                if u + 1 < UN:
                                    turn(i, u + 1)
                                elif not final(i):
                                    turn(i + 1, 0)
                                spread(i, u, tile(u))
                                if u >= 2:
                                    add_up(i, u - 2)
                                elif not (isinstance(i, int) and i == 0):
                                    add_up(i - 1, u + UN - 2)
                        steps(pe, body)
                        add_up(STEPS - 1, UN - 2)
                        add_up(STEPS - 1, UN - 1)
                    else:
                        steps(pe, lambda i: [add_up(i, u) for u in range(UN)])

        def own_peaks():
            f_in, f_v, f_go, f_g, f_t = (sem("peak_" + n) for n in ("in", "v", "go", "g", "t"))
            masked = msg.rearrange("p u j n -> p (u j n)")[:, 0:2 * HEADS * P].rearrange(
                "p (j h n) -> p j h n", j=2, h=HEADS)
            hot, low = onehot[:, 0, :, :], onehot[:, 1, :, :]
            found = small[:, 0:2 * HEADS].rearrange("p (j h) -> p j h", j=2)
            ops = 3 + 2 * HEADS + 4

            def is_wide(eng):
                return eng.value_load(wide[0:1, 0:1], min_val=0, max_val=1) > 0

            with nc.Block() as block:
                @block.sync
                def _(sp):
                    with sp.If(is_wide(sp)):
                        sp.dma_start(src_sb, src_cols).then_inc(f_in, 16)
                        sp.dma_start(dst_sb, dst_cols).then_inc(f_in, 16)

                @block.gpsimd
                def _(pool):
                    with pool.If(is_wide(pool)):
                        with pool.Fori(0, PAIRS) as n:
                            pool.wait_ge(f_v, ops * n + 2)
                            pool.sem_inc(f_go, 1)
                            for j in range(2):
                                pool.indirect_dma_start(out=got[:, 0, j, 0:AW], out_offset=None, in_=table0,
                                                        in_offset=bass.IndirectOffsetOnAxis(
                                                            ap=idx_ring[:, j:j + 1], axis=0)).then_inc(f_g, 16)

                @block.vector
                def _(dve):
                    def pair(n, t):
                        at = [1]

                        def link(ins):
                            ins.then_inc(f_v, 1)
                            at[0] += 1
                            dve.wait_ge(f_v, ops * n + at[0])

                        link(dve.tensor_copy(idx_ring[:, 0:2], src_sb[:, bass.ds(2 * n, 2)]))
                        link(dve.tensor_tensor(hot, iota_n[:, :].unsqueeze(1).broadcast_to([P, 2, P]),
                                               dst_sb[:, bass.ds(2 * n, 2)].unsqueeze(2).broadcast_to([P, 2, P]),
                                               ALU.is_equal))
                        link(dve.tensor_scalar(low, hot, FMAX, -FMAX, ALU.mult, ALU.add))
                        dve.wait_ge(f_g, 32 * n + 32)
                        for j in range(2):
                            for h in range(HEADS):
                                link(dve.scalar_tensor_tensor(
                                    out=masked[:, j, h, :], in0=hot[:, j, :],
                                    scalar=got[:, 0, j, D + h:D + h + 1], in1=low[:, j, :],
                                    op0=ALU.mult, op1=ALU.add))
                        dve.wait_ge(f_t, n + 1)
                        for j in range(2):
                            link(dve.tensor_reduce(found[:, j, :],
                                                   psum[j][:, :].rearrange("p (h n) -> p h n", h=HEADS),
                                                   AX_X, ALU.max))
                        cell = arena[:, bass.ds(t * HEADS + peak_at, HEADS)]
                        for j in range(2):
                            link(dve.tensor_tensor(cell, cell, found[:, j, :], ALU.max))

                    with dve.If(is_wide(dve)):
                        dve.wait_ge(f_in, 32)
                        dve.memset(peak, -FMAX).then_inc(f_v, 1)
                        dve.wait_ge(f_v, 1)
                        with dve.Fori(0, PAIRS // 4) as i:
                            word = dve.value_load(tpack[0:1, bass.ds(i, 1)], min_val=0, max_val=(1 << 24) - 1)
                            for u in range(4):
                                pair(4 * i + u, dve.snap((word // (1 << (6 * u))) % 64))

                @block.tensor
                def _(pe):
                    with pe.If(is_wide(pe)):
                        with pe.Fori(0, PAIRS) as n:
                            pe.wait_ge(f_v, ops * n + 4 + 2 * HEADS)
                            for j in range(2):
                                for h in range(HEADS):
                                    last = pe.transpose(cols(psum[j], h), masked[:, j, h, :], ident[:, :])
                            last.then_inc(f_t, 1)

        row_stats("ln0")

        def load_gat(sp, s):
            sp.dma_start(wraw, g0_w.rearrange("(c k) n -> k c n", c=KC)).then_inc(s, 16)
            for a, v in enumerate((g0_al, g0_ar)):
                sp.dma_start(attn[:, a, :], v.rearrange("h d -> (h d)").partition_broadcast(P)).then_inc(s, 16)

        def build_gat(dve, s):
            dve.wait_ge(s["w"], 48)
            link = Chain(dve, s["b"])
            link(dve.tensor_copy(wproj[:, :, 0:D], wraw))
            for c in range(KC):
                for a in range(2):
                    link(dve.tensor_tensor(stage_flat[:, 0:D], wraw[:, c, :], attn[:, a, :], ALU.mult))
                    link(dve.reduce_sum(wproj[:, c, D + HEADS * a:D + HEADS * (a + 1)],
                                        stage_flat[:, 0:D].rearrange("p (h d) -> p h d", h=HEADS), AX_X))

        def gat_out_act(act, s, i, u):
            k = i * TB + u
            act.wait_ge(s["f"], k + 1)
            wait(act, s["out"][u], 16 * i)
            act.copy(er_flat[:, bass.ds(k * 8, HEADS)], psum[3 + TURN[u]][:, GW:AW])
            act.copy(stage[:, u, 0:GW], psum[3 + TURN[u]][:, 0:GW]).then_inc(s["e"], 1)

        def gat_out_dve(dve, s, i, u):
            k = i * TB + u
            xs = xflat[:, bass.ds(k * D, D)]
            dve.tensor_tensor(xs, xs, y_ring[:, u, :], ALU.add).then_inc(s["h"], 1)
            dve.wait_ge(s["e"], k + 1)
            dve.tensor_copy(el_flat[:, bass.ds(k * HEADS, HEADS)], stage[:, u, D:GW]).then_inc(s["b"], 1)
            dve.tensor_scalar(stage[:, u, GW:AW], stage[:, u, D:GW], 0.2, None, ALU.mult).then_inc(s["q"], 1)

        def gat_store(sp, s, i, u):
            k = i * TB + u
            sp.wait_ge(s["q"], k + 1)
            sp.dma_start(table0[bass.ds(k * P, P), :], stage[:, u, :]).then_inc(s["out"][u], 16)

        el_flat = el_all.rearrange("p t n -> p (t n)")
        er_flat = er_u.rearrange("p t n -> p (t n)")

        def gat_rows(act, s, t, u):
            wait(act, s["h"], t - TB + 1)
            layernorm_rows(act, s, t, u)

        project("gat", AW, wproj, {"act": gat_rows},
                {"act": gat_out_act, "dve": gat_out_dve}, load_gat, 48, before=build_gat, n_before=9,
                store=gat_store)

        m_v, m_p = sem("m_v"), sem("m_p")
        with nc.Block() as block:
            @block.gpsimd
            def _(pool):
                pool.memset(acc_flat, 0.0).then_inc(m_p, 1)
                pool.wait_ge(m_v, 3)
                pool.partition_all_reduce(small[:, 8:16], small[:, 0:8], P, RMAX).then_inc(m_p, 1)
                pool.wait_ge(m_p, 2)

            @block.vector
            def _(dve):
                link = Chain(dve, m_v)
                by_head = el_all.rearrange("p t n -> p n t")
                link(dve.tensor_reduce(small[:, 0:4], by_head, AX_X, ALU.max))
                link(dve.tensor_reduce(small[:, 4:8], by_head, AX_X, ALU.min))
                link(dve.tensor_scalar(small[:, 4:8], small[:, 4:8], -1.0, None, ALU.mult))
                dve.wait_ge(m_p, 2)
                link(dve.tensor_tensor(small[:, 16:20], small[:, 8:12], small[:, 12:16], ALU.add))
                link(dve.tensor_reduce(small[:, 20:21], small[:, 16:20], AX_X, ALU.max))
                link(dve.tensor_scalar(wide[:, :], small[0:1, 20:21], SPAN, None, ALU.is_gt))
                link(dve.tensor_copy(peak, small[:, 8:12].unsqueeze(1).broadcast_to([P, NT, HEADS])))

        own_peaks()

        b_v = sem("b_v")
        with nc.Block() as block:
            @block.vector
            def _(dve):
                link = Chain(dve, b_v)
                er, low = er_u[:, :, 0:4], er_u[:, :, 4:8]
                link(dve.tensor_tensor(el_all, er, peak, ALU.add))
                link(dve.scalar_tensor_tensor(out=peak, in0=el_all, scalar=0.2, in1=el_all,
                                              op0=ALU.mult, op1=ALU.max))
                link(dve.scalar_tensor_tensor(out=low, in0=er, scalar=0.2, in1=peak, op0=ALU.mult, op1=ALU.subtract))
                link(dve.tensor_tensor(er, er, peak, ALU.subtract))
                for k in range(3):
                    link(dve.tensor_copy(er_parts[:, :, k, :], er_u[:, :, :]))
                    if k < 2:
                        link(dve.tensor_tensor(er_u[:, :, :], er_u[:, :, :], er_parts[:, :, k, :], ALU.subtract))

        walk("gat_walk", True)

        a_v, a_s, a_in = sem("a_v"), sem("a_s"), sem("a_in")
        halves = [stage[:, :, 0:D], y_ring]
        biased, added = [], []
        with nc.Block() as block:
            @block.sync
            def _(sp):
                sp.dma_start(bias_bc, g0_bias.partition_broadcast(P)).then_inc(a_in, 16)
                sp.dma_start(gate_w[:, :, :], f0_gw.rearrange("(c k) n -> k c n", c=KC)).then_inc(a_in, 16)
                sp.dma_start(gate_b[:, :], f0_gb.partition_broadcast(P)).then_inc(a_in, 16)
                sp.wait_ge(a_in, 48)

            @block.vector
            def _(dve):
                link = Chain(dve, a_v)
                den = acc[:, :, D:GW]

                def add_exp(g):
                    xs = xres[:, g * TB:(g + 1) * TB, :]
                    dve.wait_ge(a_s, 2 * g + 3)
                    link(dve.scalar_tensor_tensor(out=xs, in0=halves[g % 2], scalar=-1.0, in1=xs,
                                                  op0=ALU.add, op1=ALU.add))
                    added.append(link.n)

                link(dve.tensor_scalar(den, den, 1e-30, None, ALU.max))
                link(dve.reciprocal(den, den))
                link(dve.tensor_scalar(lnt[:, 3, :], acc[:, :, GW], 1.0, None, ALU.add))
                dve.wait_ge(a_s, 1)
                link(dve.reciprocal(dis[:, :], lnt[:, 4, :]))
                dve.wait_ge(a_in, 48)
                for g in range(NG):
                    t0, t1 = g * TB, (g + 1) * TB
                    a, xs = acc[:, t0:t1, 0:D], xres[:, t0:t1, :]
                    ah = a.rearrange("p t (h d) -> p t h d", h=HEADS)
                    link(dve.tensor_tensor(ah, ah, acc[:, t0:t1, D:GW].unsqueeze(3).broadcast_to([P, TB, HEADS, HD]),
                                           ALU.mult))
                    link(dve.tensor_tensor(a, a, bias_bc.unsqueeze(1).broadcast_to([P, TB, D]), ALU.add))
                    biased.append(link.n)
                    link(dve.scalar_tensor_tensor(out=xs, in0=a, scalar=0.0, in1=xs, op0=ALU.max, op1=ALU.add))
                    if g:
                        add_exp(g - 1)
                add_exp(NG - 1)

            @block.scalar
            def _(act):
                act.wait_ge(a_v, 3)
                act.activation(lnt[:, 4, :], lnt[:, 3, :], ACT.Sqrt).then_inc(a_s, 1)
                for g in range(NG):
                    act.wait_ge(a_v, max(biased[g], added[g - 2] if g >= 2 else 0))
                    act.activation(halves[g % 2], acc[:, g * TB:(g + 1) * TB, 0:D], ACT.Relu, scale=-1.0).then_inc(a_s, 1)
                    act.wait_ge(a_s, 2 * g + 2)
                    act.activation(halves[g % 2], halves[g % 2], ACT.Exp, scale=-1.0).then_inc(a_s, 1)

        def load_gate(w, b):
            def load(sp, s):
                sp.dma_start(gate_w[:, :, :], w.rearrange("(c k) n -> k c n", c=KC)).then_inc(s, 16)
                sp.dma_start(gate_b[:, :], b.partition_broadcast(P)).then_inc(s, 16)
            return load

        def take_logits(dve, s, i, u):
            k = i * TB + u
            dve.wait_ge(s["f"], k + 1)
            dve.tensor_tensor(logit[:, :, :].rearrange("p t e -> p (t e)")[:, bass.ds(k * NE, NE)],
                              psum[3 + TURN[u]][:, 0:NE], gate_b[:, :], ALU.add).then_inc(s["e"], 1)

        def route(tag, choices, cap):
            s_v, s_a, s_p = sem(tag + "_v"), sem(tag + "_a"), sem(tag + "_p")
            W = NT * NE
            at = [0]

            def tmp(width):
                at[0] += width
                return arena[:, at[0] - width:at[0]]

            def grid():
                return tmp(W).rearrange("p (t e) -> p t e", e=NE)

            probs, hit, chosen, tot, incl, place, within, t0 = (grid() for _ in range(8))
            oh = [grid() for _ in range(choices)]
            top = [tmp(NT) for _ in range(choices)]
            red, red2, m = tmp(NT), tmp(NT), tmp(NT)
            num, tiles_of_e, ends, start, rowbase, iota_m = (tmp(NE) for _ in range(6))
            num_i = tmp(NE).bitcast(I32)
            te = tmp(P)

            def over_e(a):
                return a.unsqueeze(2).broadcast_to([P, NT, NE])

            def over_t(a):
                return a.unsqueeze(1).broadcast_to([P, NT, NE])

            with nc.Block() as block:
                @block.scalar
                def _(act):
                    act.wait_ge(s_v, 2)
                    act.activation(probs, probs, ACT.Exp).then_inc(s_a, 1)

                @block.tensor
                def _(pe):
                    pe.wait_ge(s_p, 1)
                    flat = chosen.rearrange("p t e -> p (t e)")
                    pe.matmul(psum[0][:, 0:W], tri[:, :], flat, start=True, stop=True)
                    pe.matmul(psum[1][:, 0:W], ones[:, :], flat, start=True, stop=True).then_inc(s_p, 1)

                @block.vector
                def _(dve):
                    link = Chain(dve, s_v)
                    link(dve.tensor_reduce(red, logit[:, :, :], AX_X, ALU.max))
                    link(dve.tensor_tensor(probs, logit[:, :, :], over_e(red), ALU.subtract))
                    dve.wait_ge(s_a, 1)
                    link(dve.reduce_sum(red, probs, AX_X))
                    link(dve.reciprocal(red2, red))
                    link(dve.tensor_tensor(probs, probs, over_e(red2), ALU.mult))
                    link(dve.tensor_scalar(iota_m, iota_e[:, :], -float(NE), None, ALU.add))
                    for k in range(choices):
                        link(dve.tensor_reduce(top[k], probs, AX_X, ALU.max))
                        link(dve.tensor_tensor(hit, probs, over_e(top[k]), ALU.is_equal))
                        link(dve.tensor_tensor(hit, hit, over_t(iota_m), ALU.mult))
                        link(dve.tensor_reduce(red, hit, AX_X, ALU.min))
                        link(dve.tensor_tensor(oh[k], over_t(iota_m), over_e(red), ALU.is_equal))
                        if k + 1 < choices:
                            link(dve.scalar_tensor_tensor(out=probs, in0=oh[k], scalar=-4.0, in1=probs,
                                                          op0=ALU.mult, op1=ALU.add))
                        link(dve.tensor_tensor(oh[k], oh[k], over_e(valid[:, :]), ALU.mult))
                    if choices == 1:
                        link(dve.tensor_copy(chosen, oh[0]))
                    else:
                        link(dve.tensor_tensor(chosen, oh[0], oh[1], ALU.add))
                    dve.sem_inc(s_p, 1)
                    dve.wait_ge(s_p, 2)
                    link(dve.tensor_copy(tot, psum[1][:, 0:W].rearrange("p (t e) -> p t e", e=NE)))
                    for e in range(NE):
                        link(dve.tensor_tensor_scan(incl[:, :, e], ones[:, 0:NT], tot[:, :, e], 0.0,
                                                    ALU.mult, ALU.add))
                    link(dve.tensor_tensor(place, incl, tot, ALU.subtract))
                    link(dve.scalar_tensor_tensor(out=place, in0=psum[0][:, 0:W].rearrange("p (t e) -> p t e", e=NE),
                                                  scalar=-1.0, in1=place, op0=ALU.add, op1=ALU.add))
                    link(dve.tensor_scalar(within, place, float(cap), None, ALU.is_lt))
                    link(dve.tensor_scalar(num, incl[:, NT - 1, :], float(cap), float(P - 1), ALU.min, ALU.add))
                    link(dve.tensor_copy(num_i, num))
                    link(dve.tensor_scalar(num_i, num_i, 7, None, ALU.arith_shift_right))
                    link(dve.tensor_copy(tiles_of_e, num_i))
                    link(dve.tensor_tensor_scan(ends, ones[:, 0:NE], tiles_of_e, 0.0, ALU.mult, ALU.add))
                    link(dve.tensor_tensor(start, ends, tiles_of_e, ALU.subtract))
                    link(dve.tensor_scalar(rowbase, start, float(P), None, ALU.mult))
                    link(dve.tensor_tensor(place, place, over_t(rowbase), ALU.add))
                    for k in range(choices):
                        link(dve.tensor_tensor(t0, oh[k], within, ALU.mult))
                        link(dve.reduce_sum(m, t0, AX_X))
                        link(dve.tensor_tensor(t0, t0, place, ALU.mult))
                        link(dve.reduce_sum(red, t0, AX_X))
                        link(dve.tensor_copy(slot[:, 2 * k + 1, :], red))
                        link(dve.tensor_scalar(red2, m, -float(1 << 20), float(1 << 20), ALU.mult, ALU.add))
                        link(dve.tensor_tensor(slot[:, 2 * k, :], red, red2, ALU.add))
                        if choices == 1:
                            link(dve.tensor_tensor(wgt[:, 0, :], top[0], m, ALU.mult))
                    if choices == 2:
                        link(dve.tensor_tensor(red, top[0], top[1], ALU.add))
                        link(dve.reciprocal(red2, red))
                        for k in range(2):
                            link(dve.tensor_tensor(wgt[:, k, :], top[k], red2, ALU.mult))
                    link(dve.tensor_scalar(te, iota_n[:, :], start[:, 1:2], None, ALU.is_ge))
                    for e in range(2, NE):
                        link(dve.scalar_tensor_tensor(out=te, in0=iota_n[:, :], scalar=start[:, e:e + 1], in1=te,
                                                      op0=ALU.is_ge, op1=ALU.add))
                    link(dve.tensor_copy(tile_e[:, :], te[0:1, :]))

        def dispatch(tag, choices, tiles, w2):
            s_w2 = sem(tag + "_w2")
            s_go = sem(tag + "_go")
            s_out = [sem(f"{tag}_s{u}") for u in range(TB)]
            with nc.Block() as block:
                @block.sync
                def _(sp):
                    for e in range(NE):
                        sp.dma_start(w2_sb[:, e, :, :], w2[e].rearrange("(c k) d -> k c d", c=FC)).then_inc(s_w2, 16)
                    sp.wait_ge(s_w2, 16 * NE)

                @block.scalar
                def _(act):
                    with act.Fori(0, NT) as t:
                        act.activation(arena[:, bass.ds(t * D + y_at, D)], xflat[:, bass.ds(t * D, D)], ACT.Identity,
                                       bias=own(nmr, t), scale=own(rstd, t)).then_inc(s_go, 1)

                @block.gpsimd
                def _(pool):
                    for t in range(NT):
                        pool.wait_ge(s_go, t + 1)
                        wait(pool, s_out[t % TB], 16 * choices * (t // TB))
                        for k in range(choices):
                            pool.indirect_dma_start(
                                out=expert_in, out_offset=bass.IndirectOffsetOnAxis(
                                    ap=slot[:, 2 * k, t:t + 1], axis=0),
                                in_=y_all[:, t * D:(t + 1) * D], in_offset=None,
                                bounds_check=tiles * P - 1, oob_is_err=False).then_inc(s_out[t % TB], 16)
                    for u in range(TB):
                        pool.wait_ge(s_out[u], 16 * choices * NG)

        def experts(tag, tiles, w1, b1, b2, func, affine):
            s_w, s_b, s_bt, s_t, s_x, s_h, s_hm, s_y, s_yo, s_go = (
                sem(tag + "_" + n) for n in ("w", "b", "bt", "t", "x", "h", "hm", "y", "yo", "go"))
            s_in = [sem(f"{tag}_in{u}") for u in range(2)]
            s_w1 = [sem(f"{tag}_w1{u}") for u in range(2)]
            w1_rows = w1.rearrange("e k f -> (e k) f")
            s_out = [sem(f"{tag}_out{u}") for u in range(2)]
            raw = y_out.rearrange("p s d -> p (s d)")
            n_raw = 3 if affine else 1
            half = tiles // 2

            def steps(eng, body):
                body(0)
                with eng.Fori(1, half - 1) as i:
                    body(i)
                body(half - 1)

            def first(k):
                return isinstance(k, int) and k == 0

            def last_(k):
                return isinstance(k, int) and k == tiles - 1

            with nc.Block() as block:
                @block.sync
                def _(sp):
                    sp.dma_start(raw[0:NE * FC, 0:P], b1.rearrange("e (c k) -> (e c) k", k=P)).then_inc(s_b, 16)
                    if affine:
                        for a, v in enumerate(affine):
                            sp.dma_start(raw[0:NE * KC, P * (a + 1):P * (a + 2)],
                                         v.rearrange("e (c k) -> (e c) k", k=P)).then_inc(s_b, 16)
                    sp.dma_start(b2_bc, b2.rearrange("e d -> (e d)").partition_broadcast(P)).then_inc(s_w, 16)

                    def load(k, u):
                        wait(sp, s_t, k - 1)
                        sp.dma_start(x_in[:, u, :], expert_in[bass.ds(k * P, P), :]).then_inc(s_in[u], 16)

                    def load_w1(k, u):
                        e = sp.value_load(tile_e[0:1, bass.ds(k, 1)], min_val=0, max_val=NE - 1)
                        wait(sp, s_h, 2 * (k - 1))
                        sp.dma_start(w1_ring[:, u, :, :],
                                     w1_rows[bass.ds(e * D, D), :].rearrange("(c k) f -> k c f", c=KC)
                                     ).then_inc(s_w1[u], 16)

                    for u in range(2):
                        load(u, u)
                        load_w1(u, u)
                    def body(i):
                        for u in range(2):
                            k = 2 * i + u
                            if not (isinstance(k, int) and k + 2 >= tiles):
                                load(k + 2, u)
                                load_w1(k + 2, u)
                    steps(sp, body)

                @block.gpsimd
                def _(pool):
                    def store(k, u):
                        pool.wait_ge(s_yo, k + 1)
                        pool.sem_inc(s_go, 1)
                        pool.dma_start(expert_out[bass.ds(k * P, P), :], y_out[:, u, :]).then_inc(s_out[u], 16)

                    with pool.Fori(0, half) as i:
                        for u in range(2):
                            store(2 * i + u, u)
                    for u in range(2):
                        pool.wait_ge(s_out[u], 16 * half)

                @block.vector
                def _(dve):
                    dve.wait_ge(s_w, 16)
                    dve.wait_ge(s_bt, 1)
                    dve.tensor_copy(b1_sb[:, :, :].rearrange("p e c -> p (e c)"), psum[0][:, 0:NE * FC]).then_inc(s_bt, 1)
                    if affine:
                        for a, v in enumerate((lg_sb, lb_sb)):
                            dve.tensor_copy(v[:, :, :].rearrange("p e c -> p (e c)"),
                                            psum[1 + a][:, 0:NE * KC]).then_inc(s_bt, 1)
                        dve.wait_ge(s_bt, 4)

                    def rows_in(k, u):
                        dve.wait_ge(s_t, k + 1)
                        wait(dve, s_h, 2 * (k - 1))
                        if affine:
                            e = dve.value_load(tile_e[0:1, bass.ds(k, 1)], min_val=0, max_val=NE - 1)
                            for c in range(KC):
                                last = dve.tensor_scalar(
                                    cols(yt_ring[:, u, :], c), cols(psum[4 + u], c),
                                    lg_sb[:, :, :].rearrange("p e c -> p (e c)")[:, bass.ds(e * KC + c, 1)],
                                    lb_sb[:, :, :].rearrange("p e c -> p (e c)")[:, bass.ds(e * KC + c, 1)],
                                    ALU.mult, ALU.add)
                        else:
                            last = dve.tensor_copy(yt_ring[:, u, :], psum[4 + u][:, 0:D])
                        last.then_inc(s_x, 1)

                    def rows_out(k, u):
                        dve.wait_ge(s_y, k + 1)
                        wait(dve, s_out[u], 8 * (k - u))
                        e = dve.value_load(tile_e[0:1, bass.ds(k, 1)], min_val=0, max_val=NE - 1)
                        dve.tensor_tensor(y_out[:, u, :], psum[6 + u][:, 0:D],
                                          arena[:, bass.ds(e * D + W2W + 2 * KC * FF, D)], ALU.add).then_inc(s_yo, 1)

                    rows_in(0, 0)

                    def body(i):
                        for u in range(2):
                            k = 2 * i + u
                            if not last_(k):
                                rows_in(k + 1, 1 - u)
                            if not first(k):
                                rows_out(k - 1, 1 - u)
                    steps(dve, body)
                    rows_out(tiles - 1, 1)

                @block.scalar
                def _(act):
                    act.wait_ge(s_bt, 2)

                    def body(i):
                        for u in range(2):
                            k = 2 * i + u
                            e = act.value_load(tile_e[0:1, bass.ds(k, 1)], min_val=0, max_val=NE - 1)
                            wait(act, s_y, k - 1)
                            for h in range(2):
                                act.wait_ge(s_h, 2 * k + h + 1)
                                for c in range(h * FC // 2, (h + 1) * FC // 2):
                                    last = act.activation(
                                        hmid[:, u, c, :], psum[2 * u + h][:, (c % 4) * P:(c % 4 + 1) * P], func,
                                        bias=b1_sb[:, :, :].rearrange("p e c -> p (e c)")[:, bass.ds(e * FC + c, 1)])
                                last.then_inc(s_hm, 1)
                    steps(act, body)

                @block.tensor
                def _(pe):
                    pe.wait_ge(s_b, 16 * n_raw)
                    last = pe.transpose(psum[0][:, 0:NE * FC], raw[0:NE * FC, 0:P], ident[0:NE * FC, 0:NE * FC])
                    for a in range(n_raw - 1):
                        last = pe.transpose(psum[1 + a][:, 0:NE * KC], raw[0:NE * KC, P * (a + 1):P * (a + 2)],
                                            ident[0:NE * KC, 0:NE * KC])
                    last.then_inc(s_bt, 1)
                    pe.wait_ge(s_bt, 1 + n_raw)
                    pe.wait_ge(s_w, 16)

                    def turn(k, u):
                        pe.wait_ge(s_in[u], 8 * (k - u) + 16)
                        wait(pe, s_x, k - 1)
                        for c in range(KC):
                            last = pe.transpose(cols(psum[4 + u], c), cols(x_in[:, u, :], c), ident[:, :])
                        last.then_inc(s_t, 1)

                    def layer1(k, u):
                        pe.wait_ge(s_x, k + 1)
                        pe.wait_ge(s_w1[u], 8 * (k - u) + 16)
                        for h in range(2):
                            wait(pe, s_hm, 2 * (k - 2) + h + 1)
                            for f in range(h * FC // 2, (h + 1) * FC // 2):
                                for c in range(KC):
                                    last = pe.matmul(psum[2 * u + h][:, (f % 4) * P:(f % 4 + 1) * P],
                                                     w1_ring[:, u, c, f * P:(f + 1) * P],
                                                     cols(yt_ring[:, u, :], c),
                                                     start=(c == 0), stop=(c == KC - 1))
                            last.then_inc(s_h, 1)

                    def layer2(k, u, e):
                        pe.wait_ge(s_hm, 2 * k + 2)
                        wait(pe, s_yo, k - 1)
                        for f in range(FC):
                            last = pe.matmul(psum[6 + u][:, 0:D], hmid[:, u, f, :],
                                             arena[:, bass.ds(e * FC * D + f * D, D)],
                                             start=(f == 0), stop=(f == FC - 1))
                        last.then_inc(s_y, 1)

                    turn(0, 0)

                    def expert(k):
                        return pe.value_load(tile_e[0:1, bass.ds(k, 1)], min_val=0, max_val=NE - 1)

                    def body(i):
                        for u in range(2):
                            k = 2 * i + u
                            e = None if first(k) else expert(k - 1)
                            layer1(k, u)
                            if not last_(k):
                                turn(k + 1, 1 - u)
                            if not first(k):
                                layer2(k - 1, 1 - u, e)
                    steps(pe, body)
                    layer2(tiles - 1, 1, expert(tiles - 1))

        def combine(tag, choices, tiles, write_out):
            s_v, s_done, s_out, s_k = (sem(tag + "_" + n) for n in ("v", "done", "out", "k"))
            s_g = [sem(f"{tag}_g{u}") for u in range(TB)]
            picks = [pick_a, pick_b][:choices]
            with nc.Block() as block:
                @block.scalar
                def _(act):
                    if choices == 1:
                        for t in range(NT):
                            act.wait_ge(s_g[t % TB], 16 * (t // TB + 1))
                            act.activation(pick_a[:, t, :], pick_a[:, t, :], ACT.Copy,
                                           scale=wgt[:, 0, t:t + 1]).then_inc(s_k, 1)

                @block.gpsimd
                def _(pool):
                    for t in range(NT):
                        wait(pool, s_g[t % TB], 16 * choices * (t // TB))
                        for k in range(choices):
                            pool.indirect_dma_start(
                                out=picks[k][:, t, :], out_offset=None, in_=expert_out[0:tiles * P, :],
                                in_offset=bass.IndirectOffsetOnAxis(ap=slot[:, 2 * k + 1, t:t + 1], axis=0)
                                ).then_inc(s_g[t % TB], 16)

                @block.vector
                def _(dve):
                    if choices == 1:
                        zero = arena[:, clean_at:clean_at + 1]
                        near = arena[:, clean_at + 8 + TB * D:clean_at + 8 + 2 * TB * D]
                        mask = arena[:, clean_at + 8:clean_at + 8 + TB * D].bitcast(I32)
                        link = Chain(dve, s_v)
                        link(dve.memset(zero, 0.0))
                        for g in range(NG):
                            y = arena[:, g * TB * D:(g + 1) * TB * D]
                            dve.wait_ge(s_k, (g + 1) * TB)
                            link(dve.tensor_tensor(mask, y, y, ALU.not_equal))
                            link(dve.copy_predicated(y, mask, zero.broadcast_to([P, TB * D])))
                            link(dve.tensor_scalar(near, y, 1.0e4, -1.0e4, ALU.min, ALU.max))
                            link(dve.tensor_scalar(mask, y, 0.0, 0.0, ALU.mult, ALU.not_equal))
                            link(dve.copy_predicated(y, mask, near))
                            xs = xflat[:, g * TB * D:(g + 1) * TB * D]
                            link(dve.tensor_tensor(xs, xs, y, ALU.add))
                    else:
                        def body(i):
                            for u in range(TB):
                                t = i * TB + u
                                a, b = (arena[:, bass.ds(t * D + k * NT * D, D)] for k in range(2))
                                xs = xflat[:, bass.ds(t * D, D)]
                                dve.wait_ge(s_g[u], 32 * (i + 1))
                                dve.tensor_scalar(a, a, own(wgt[:, 0, :], t), None, ALU.mult).then_inc(s_v, 1)
                                dve.wait_ge(s_v, 2 * t + 1)
                                dve.scalar_tensor_tensor(out=b, in0=b, scalar=own(wgt[:, 1, :], t), in1=a,
                                                         op0=ALU.mult, op1=ALU.add).then_inc(s_v, 1)
                                dve.wait_ge(s_v, 2 * t + 2)
                                dve.tensor_tensor(xs, xs, b, ALU.add).then_inc(s_done, 1)
                        rolled(dve, NG, body)

                @block.sync
                def _(sp):
                    if write_out:
                        for g in range(NG):
                            sp.wait_ge(s_done, (g + 1) * TB)
                            hi = min((g + 1) * TB, NT - 1)
                            sp.dma_start(rows(out, g * TB, hi), xres[:, g * TB:hi, :]).then_inc(s_out, 16)
                        sp.dma_start(out[(NT - 1) * P:N, :], xres[0:LAST, NT - 1, :]).then_inc(s_out, 16)
                        sp.wait_ge(s_out, 16 * (NG + 1))

        def load_w(w):
            def load(sp, s):
                sp.dma_start(wproj[:, :, 0:D], w.rearrange("(c k) n -> k c n", c=KC)).then_inc(s, 16)
            return load

        def gcn_out(act, s, i, u):
            k = i * TB + u
            act.wait_ge(s["f"], k + 1)
            act.activation(arena[:, bass.ds(k * AW, D)], psum[3 + TURN[u]][:, 0:D], ACT.Copy,
                           scale=own(dis[:, :], k)).then_inc(s["e"], 1)

        def gcn_store(sp, s, i, u):
            k = i * TB + u
            sp.wait_ge(s["e"], k + 1)
            sp.dma_start(table1[bass.ds(k * P, P), :], arena[:, bass.ds(k * AW, D)]).then_inc(s["out"][u], 16)

        def batchnorm_rows(dve, s, t, u):
            wait(dve, s["t"], t - TB + 1)
            dve.tensor_tensor(y_ring[:, u, :], arena[:, bass.ds(t * AW, D)], bn_g, ALU.mult).then_inc(s["b"], 1)
            dve.wait_ge(s["b"], t + 1)
            dve.tensor_tensor(y_ring[:, u, :], y_ring[:, u, :], bn_b, ALU.add).then_inc(s["y"], 1)

        def batch_stats(tag, b, g, bt, add_to_x):
            s_in, s_z, s_r, s_m, s_v, s_sq, s_c, s_x = (
                sem(tag + "_" + n) for n in ("in", "z", "r", "m", "v", "sq", "c", "x"))
            mu = stage[:, 0, 0:D]

            def group(i):
                return arena[:, bass.ds(i * TB * AW, TB * AW)].rearrange("p (t d) -> p t d", t=TB)[:, :, 0:D]

            def column_sums(pe, bank, source, ready, count):
                for g_ in range(NG):
                    pe.wait_ge(ready, count(g_))
                    for u in range(TB):
                        t = g_ * TB + u
                        r = LAST if t == NT - 1 else P
                        last = pe.matmul(psum[bank][:, 0:D], ones[0:r, :], source(t, u)[0:r, :],
                                         start=(t == 0), stop=(t == NT - 1))
                    last.then_inc(s_m, 1)

            with nc.Block() as block:
                @block.sync
                def _(sp):
                    sp.dma_start(bias_bc, b.partition_broadcast(P)).then_inc(s_in, 16)
                    sp.dma_start(bn_g, g.partition_broadcast(P)).then_inc(s_in, 16)
                    sp.dma_start(bn_b, bt.partition_broadcast(P)).then_inc(s_in, 16)

                @block.vector
                def _(dve):
                    dve.wait_ge(s_in, 48)
                    with dve.Fori(0, NG) as i:
                        for u in range(TB):
                            t = i * TB + u
                            a = arena[:, bass.ds(t * AW, D)]
                            dve.scalar_tensor_tensor(out=a, in0=a, scalar=own(dis[:, :], t), in1=bias_bc,
                                                     op0=ALU.mult, op1=ALU.add).then_inc(s_z, 1)
                    if add_to_x:
                        for g_ in range(NG):
                            xs = xres[:, g_ * TB:(g_ + 1) * TB, :]
                            dve.tensor_tensor(xs, xs, bn_b.unsqueeze(1).broadcast_to([P, TB, D]),
                                              ALU.add).then_inc(s_x, 1)
                    dve.wait_ge(s_m, NG)
                    link = Chain(dve, s_v)
                    link(dve.tensor_scalar(mu, psum[0][:, 0:D], 1.0 / N, None, ALU.mult))
                    with dve.Fori(0, NG) as i:
                        a = group(i)
                        dve.tensor_tensor(a, a, mu.unsqueeze(1).broadcast_to([P, TB, D]), ALU.subtract).then_inc(s_c, 1)
                    dve.wait_ge(s_m, 2 * NG)
                    link(dve.tensor_scalar(mu, psum[1][:, 0:D], 1.0 / N, None, ALU.mult))
                    dve.wait_ge(s_sq, NG + 1)
                    link(dve.reciprocal(mu, mu))
                    link(dve.tensor_tensor(bn_g, bn_g, mu, ALU.mult))
                    if add_to_x:
                        dve.wait_ge(s_x, NG)
                        for g_ in range(NG):
                            a = acc[:, g_ * TB:(g_ + 1) * TB, 0:D]
                            xs = xres[:, g_ * TB:(g_ + 1) * TB, :]
                            link(dve.tensor_tensor(a, a, bn_g.unsqueeze(1).broadcast_to([P, TB, D]), ALU.mult))
                            link(dve.tensor_tensor(xs, xs, a, ALU.add))

                @block.scalar
                def _(act):
                    with act.Fori(0, NG) as i:
                        act.wait_ge(s_z, (i + 1) * TB)
                        act.activation(group(i), group(i), ACT.Relu).then_inc(s_r, 1)
                    for g_ in range(NG):
                        act.wait_ge(s_c, g_ + 1)
                        if g_:
                            act.wait_ge(s_m, NG + g_)
                        act.activation(y_ring, acc[:, g_ * TB:(g_ + 1) * TB, 0:D], ACT.Square).then_inc(s_sq, 1)
                    act.wait_ge(s_v, 2)
                    act.activation(mu, mu, ACT.Sqrt, bias=eps[:, 0:1]).then_inc(s_sq, 1)

                @block.tensor
                def _(pe):
                    column_sums(pe, 0, lambda t, u: acc[:, t, 0:D], s_r, lambda g_: g_ + 1)
                    column_sums(pe, 1, lambda t, u: y_ring[:, u, :], s_sq, lambda g_: g_ + 1)

        row_stats("ln1")
        project("gate0", NE, gate_w, {"act": layernorm_rows}, {"dve": take_logits}, load_gate(f0_gw, f0_gb), 32)
        route("route0", 1, CAP)
        dispatch("send0", 1, TILES0, f0_w2)
        experts("ffn0", TILES0, f0_w1, f0_b1, f0_b2, ACT.Relu, None)
        combine("back0", 1, TILES0, False)

        reuse_semaphores()
        row_stats("ln2")
        project("gcn0", D, wproj, {"act": layernorm_rows}, {"act": gcn_out}, load_w(g1_w0), 16, store=gcn_store)
        walk("gcn0_walk", False)
        batch_stats("bn0", g1_b0, g1_g0, g1_bt0, False)
        project("gcn1", D, wproj, {"dve": batchnorm_rows}, {"act": gcn_out}, load_w(g1_w1), 16, store=gcn_store)
        walk("gcn1_walk", False)
        batch_stats("bn1", g1_b1, g1_g1, g1_bt1, True)

        reuse_semaphores()
        row_stats("ln3")
        project("gate1", NE, gate_w, {"act": layernorm_rows}, {"dve": take_logits}, load_gate(f1_wr, f1_br), 32)
        route("route1", 2, 1 << 20)
        dispatch("send1", 2, TILES1, f1_w2)
        experts("ffn1", TILES1, f1_w1, f1_b1, f1_b2, ACT.Gelu, (f1_lg, f1_lb))
        combine("back1", 2, TILES1, True)


_INS = ["x", "src", "dst", "L0_gnn_W", "L0_gnn_attn_l", "L0_gnn_attn_r", "L0_gnn_bias", "L0_ffn_gate_w",
        "L0_ffn_gate_b", "L0_ffn_w1", "L0_ffn_b1", "L0_ffn_w2", "L0_ffn_b2", "L1_gnn_W0", "L1_gnn_b0",
        "L1_gnn_g0", "L1_gnn_bt0", "L1_gnn_W1", "L1_gnn_b1", "L1_gnn_g1", "L1_gnn_bt1", "L1_ffn_Wr",
        "L1_ffn_br", "L1_ffn_ln_g", "L1_ffn_ln_b", "L1_ffn_W1", "L1_ffn_b1", "L1_ffn_W2", "L1_ffn_b2"]


def kernel(**inputs):
    import concourse.bacc as bacc
    from concourse.bass_utils import run_bass_kernel_spmd

    nc = bacc.Bacc("TRN2", target_bir_lowering=False, num_devices=1)
    arrays, args = {}, []
    for name in _INS:
        a = np.ascontiguousarray(inputs[name])
        arrays[f"in_{name}"] = a
        args.append(nc.dram_tensor(f"in_{name}", a.shape, mybir.dt.from_np(a.dtype), kind="ExternalInput").ap())
    args.append(nc.dram_tensor("out_x", (N, D), F32, kind="ExternalOutput").ap())
    build(nc, *args)
    return run_bass_kernel_spmd(nc, [arrays], core_ids=[0]).results[0]["out_x"]
```
